# Optimizing a Trainium2 kernel written in Bass

```python
import numpy as np
import jax
import jax.numpy as jnp

def _softmax(x, axis=-1):
    return jax.nn.softmax(x, axis=axis)

def _gelu(x):
    return jax.nn.gelu(x, approximate=True)

def _silu(x):
    return jax.nn.silu(x)

def _sigmoid(x):
    return jax.nn.sigmoid(x)

def _layernorm(x, axis=-1, eps=1e-05):
    m = jnp.mean(x, axis=axis, keepdims=True)
    v = jnp.var(x, axis=axis, keepdims=True)
    return (x - m) / jnp.sqrt(v + eps)

def _scatter_add(tgt, idx, src, axis=0):
    return tgt.at[idx].add(src)

def _segment_sum(src, seg, n):
    return jax.ops.segment_sum(src, seg, n)
kernel_name = 'mk_adj_preln_d1_adj_r2_0c1687'

def setup_inputs(seed: int=0):
    np.random.seed(seed)
    _w = jnp.asarray

    def _rec_inputs():
        import jax
        import jax.numpy as jnp
        _gk = jax.random.key(seed)
        x = 7.22e-05 + 1 * jax.random.normal(jax.random.fold_in(_gk, 1), (8, 1024, 128), jnp.float32)
        _w = (1.0 + jnp.arange(1024, dtype=jnp.float32)) ** (-0.5)
        _w = _w / _w.mean()
        _pij = jnp.clip(0.015625 * _w[:, None] * _w[None, :], 0.0, 1.0)
        _a = jax.random.uniform(jax.random.fold_in(_gk, 2), (8, 1024, 1024)) < _pij
        adj = _a.astype(jnp.int32)
        return (x, adj)
    x, adj = _rec_inputs()

    def _L0_gnn_setup():
        import jax, jax.numpy as jnp
        import numpy as np
        B, N, IN_F, OUT_F = (32, 512, 128, 128)
        ALPHA = 0.2
        NEG_INF = -9000000000000000.0
        key = jax.random.key(seed)
        k1, k2, k3, k4 = jax.random.split(key, 4)
        h = jax.random.normal(k1, (B, N, IN_F), dtype=jnp.float32)
        adj = jax.random.randint(k2, (B, N, N), 0, 2, dtype=jnp.int32)
        W = jax.random.normal(k3, (OUT_F, IN_F), dtype=jnp.float32) * 0.05
        a = jax.random.normal(k4, (1, 2 * OUT_F), dtype=jnp.float32) * 0.05
        return {'h': h, 'adj': adj, 'W': W, 'a': a}
    _L0_gnn_all = _L0_gnn_setup()
    _L0_gnn_in = {k: v for k, v in _L0_gnn_all.items() if k in ('W', 'a')}
    del _L0_gnn_all
    return {'x': x, 'adj': adj, 'L0_gnn_W': _L0_gnn_in['W'], 'L0_gnn_a': _L0_gnn_in['a']}

def reference(x, adj, L0_gnn_W, L0_gnn_a):
    import jax
    import jax.numpy as jnp

    def _L0_gnn_ref(h, adj, W, a):
        import jax, jax.numpy as jnp
        import numpy as np
        B, N, IN_F, OUT_F = (32, 512, 128, 128)
        ALPHA = 0.2
        NEG_INF = -9000000000000000.0
        Wh = jnp.einsum('bni,oi->bno', h, W)
        a1 = a[0, :OUT_F]
        a2 = a[0, OUT_F:]
        si = Wh @ a1
        sj = Wh @ a2
        e = jax.nn.leaky_relu(si[:, :, None] + sj[:, None, :], negative_slope=ALPHA)
        attention = jnp.where(adj > 0, e, NEG_INF)
        attention = jax.nn.softmax(attention, axis=-1)
        h_prime = jnp.einsum('bij,bjo->bio', attention, Wh)
        return jax.nn.elu(h_prime)
    h = jnp.maximum(_layernorm(x, axis=-1), 0.0)
    x = x + _L0_gnn_ref(h, adj, L0_gnn_W, L0_gnn_a)
    return x

_drawn_inputs = setup_inputs


def setup_inputs(seed=0):
    import zlib

    import numpy as np

    out = dict(_drawn_inputs(seed))
    spreads = {}
    factors = {'L0_gnn_a': 4.715}
    for name, (base, spread) in spreads.items():
        noise = np.random.default_rng([zlib.crc32(name.encode()), seed]).standard_normal(out[name].shape)
        drawn = base * np.exp(spread * noise) if base else spread * noise
        out[name] = jnp.asarray(drawn.astype(out[name].dtype))
    for name, factor in factors.items():
        out[name] = (out[name] * factor).astype(out[name].dtype)
    return out
```

```python
import concourse.bass as bass
from concourse import mybir
from contextlib import ExitStack

FP32 = mybir.dt.float32
I32 = mybir.dt.int32
ALU = mybir.AluOpType
ACT = mybir.ActivationFunctionType
AX = mybir.AxisListType


def graph_attention_kernel(nc, x, adj, w, a, out):
    BATCHES, N, D = x.shape
    P = 128
    TILES = N // P
    HT = TILES // 2
    HN = N // 2
    UW = D + 2
    NW = D + 1
    ALPHA = 0.2
    EPS = 1e-5
    CONSTANTS = 10
    TINY = 2.0 ** -100
    SAFE_SCORE = 30.0
    LOOPS = (BATCHES - 2) // 2
    FACTOR = 1.0 - ALPHA
    WH_FILLS = ((0, 3), (3, 6), (6, 8))
    FILLS = 4 + len(WH_FILLS)

    x_t = x.rearrange("b (t p) d -> b p t d", p=P)
    out_t = out.rearrange("b (t p) d -> b p t d", p=P)
    adj_t = adj.rearrange("b (t p) j -> b p t j", p=P)

    ctx = ExitStack()
    with ctx:
        def sb(name, shape, dt=FP32):
            return ctx.enter_context(nc.sbuf_tensor(name, shape, dt))

        def sem(name):
            return ctx.enter_context(nc.semaphore(name))

        adj_rows = sb("adj_rows", [P, 4, HT, N], I32)
        weights = sb("weights", [P, 2, TILES, HN])
        xs = sb("xs", [P, BATCHES, TILES * D])
        xc = sb("xc", [P, TILES * D])
        xsq = sb("xsq", [P, TILES * D])
        hT = sb("hT", [P, N])
        wh = sb("wh", [P, 2, TILES, D + 3])
        g_row = sb("g_row", [P, 2, N])
        b_col = sb("b_col", [P, 2, TILES])
        d_col = sb("d_col", [P, 2, TILES])
        tiny_row = sb("tiny_row", [P, 2, NW])
        num = sb("num", [P, 2, HT, NW])
        rden = sb("rden", [P, 2, HT])
        y = sb("y", [P, 2, HT * D])
        ey = sb("ey", [P, 2, HT * D])
        res = sb("res", [P, 2, HT * D])
        ident = sb("ident", [P, P])
        ones = sb("ones", [P, P])
        w_rows = sb("w_rows", [P, D])
        a_cols = sb("a_cols", [P, 2])
        u = sb("u", [P, UW])
        u1_wide = sb("u1_wide", [P, P])
        hsum = sb("hsum", [P, 2])
        hsum_wide = sb("hsum_wide", [P, P])
        rsum = sb("rsum", [P, TILES])
        nmean = sb("nmean", [P, TILES])
        ssq = sb("ssq", [P, TILES])
        var = sb("var", [P, TILES])
        rstd = sb("rstd", [P, TILES])
        neg_half = sb("neg_half", [P, TILES])
        inv_d = sb("inv_d", [P, TILES])
        neg_inv_d = sb("neg_inv_d", [P, TILES])
        eps = sb("eps", [P, TILES])
        sjmax = sb("sjmax", [P, 1])
        m_all = sb("m_all", [P, 1])
        shift = sb("shift", [P, 3])
        shift_f = sb("shift_f", [P, 3])
        smax = sb("smax", [P, BATCHES])

        adjT = [ctx.enter_context(nc.psum_tensor(f"adjT{i}", [P, 2, HN], FP32)) for i in range(2)]
        nump = [ctx.enter_context(nc.psum_tensor(f"nump{i}", [P, 512], FP32)) for i in range(2)]
        prep = [ctx.enter_context(nc.psum_tensor(f"prep{i}", [P, 512], FP32)) for i in range(2)]

        def dma_sems(name, n):
            return [sem(f"{name}{i}") for i in range(n)]

        zeroed, ident_ready, consts_ready = sem("zeroed"), sem("ident_ready"), sem("consts_ready")
        weights_loaded = sem("weights_loaded")
        setup_products = sem("setup_products")
        u_ready = sem("u_ready")
        adj_loaded = dma_sems("adj_loaded", 4)
        x_loaded = dma_sems("x_loaded", 3)
        rsum_ready, nmean_ready, xc_ready = sem("rsum_ready"), sem("nmean_ready"), sem("xc_ready")
        xsq_ready, ssq_ready, var_ready = sem("xsq_ready"), sem("ssq_ready"), sem("var_ready")
        rstd_ready, hn_ready = sem("rstd_ready"), sem("hn_ready")
        prep_filled = sem("prep_filled")
        prep_drained = sem("prep_drained")
        hsum_ready = sem("hsum_ready")
        sjmax_ready, m_ready, shift_ready = sem("sjmax_ready"), sem("m_ready"), sem("shift_ready")
        m_filled = sem("m_filled")
        gbd_ready = sem("gbd_ready")
        adjT_ready = sem("adjT_ready")
        e_ready = sem("e_ready")
        masked = sem("masked")
        num_summed = sem("num_summed")
        num_copied = sem("num_copied")
        rden_ready, y_ready, neg_ready = sem("rden_ready"), sem("y_ready"), sem("neg_ready")
        ey_ready, elu_ready, res_ready = sem("ey_ready"), sem("elu_ready"), sem("res_ready")
        stored = dma_sems("stored", 2)

        block = ctx.enter_context(nc.Block())

        def fixed(n):
            return n, n % 2, n // 2

        def looped(k, c):
            return 2 * k + c, c % 2, k + c // 2

        def wait(eng, semaphore, count):
            if not isinstance(count, int) or count > 0:
                eng.wait_ge(semaphore, count)

        def schedule(eng, first, second, prologue, epilogue=None):
            prologue()
            first(fixed(0), prep=True, prev=False)
            with eng.Fori(0, LOOPS) as k:
                for c in range(2):
                    second(looped(k, c), looped(k, c + 1), looped(k, c + 2))
                    first(looped(k, c + 1), prep=True, prev=True)
            second(fixed(BATCHES - 2), fixed(BATCHES - 1), None)
            first(fixed(BATCHES - 1), prep=False, prev=True)
            second(fixed(BATCHES - 1), None, None)
            if epilogue:
                epilogue()

        def x_of(n, t0, t1):
            return xs[:, bass.ds(n, 1), t0 * D:t1 * D].rearrange("p o f -> p (o f)")

        def tiles(ap):
            return ap.rearrange("p (t d) -> p t d", d=D)

        def spread(ap, n):
            return ap.unsqueeze(2).to_broadcast([P, n, D])

        def next_of(b):
            return b[0] + 1, 1 - b[1]

        @block.sync
        def _(sp):
            def load_x(n0, n1, s):
                sp.dma_start(xs[:, n0:n1, :].rearrange("p b (t d) -> p b t d", d=D),
                             x_t[n0:n1].rearrange("b p t d -> p b t d")).then_inc(x_loaded[s], 16)

            def load_adj(n, par, half):
                src = adj_t[bass.ds(n, 1), :, half * HT:(half + 1) * HT, :].rearrange("o p t j -> p (o t) j")
                sp.dma_start(adj_rows[:, 2 * par + half], src).then_inc(adj_loaded[2 * par + half], 16)

            def store(n, half):
                sp.wait_ge(res_ready, 2 * n + half + 1)
                dst = out_t[bass.ds(n, 1), :, half * HT:(half + 1) * HT, :].rearrange("o p t d -> p (o t) d")
                sp.dma_start(dst, tiles(res[:, half])).then_inc(stored[half], 16)

            def prologue():
                load_x(0, 1, 0)
                sp.dma_start(w_rows[:, :], w).then_inc(weights_loaded, 16)
                with nc.allow_non_contiguous_dma(reason="a is 256 numbers, turned into two columns"):
                    sp.dma_start(a_cols[:, :], a.rearrange("o (c p) -> p (o c)", p=P)).then_inc(weights_loaded, 16)
                load_adj(0, 0, 0)
                load_x(1, 2, 1)
                load_adj(0, 0, 1)
                load_adj(1, 1, 0)
                load_x(2, BATCHES, 2)
                load_adj(1, 1, 1)

            def first(b, prep, prev):
                if prev:
                    store(b[0] - 1, 1)

            def second(b, after, ahead):
                if ahead:
                    for half in range(2):
                        sp.wait_ge(adjT_ready, 8 * b[0] + 4 * half + 4)
                        load_adj(ahead[0], ahead[1], half)
                store(b[0], 0)

            def epilogue():
                store(BATCHES - 1, 1)
                for half in range(2):
                    sp.wait_ge(stored[half], 16 * BATCHES)

            schedule(sp, first, second, prologue, epilogue)

        @block.gpsimd
        def _(pool):
            def constants():
                pool.wait_ge(consts_ready, CONSTANTS)

            def centre(n, x_sem):
                wait(pool, prep_filled, FILLS * (n - 1) + 2)
                pool.wait_ge(rsum_ready, n + 1)
                pool.wait_ge(x_loaded[x_sem], 16)
                nc.gpsimd.tensor_tensor(nmean[:, :], rsum[:, :], neg_inv_d[:, :], ALU.mult).then_inc(nmean_ready, 1)
                pool.wait_ge(nmean_ready, n + 1)
                nc.gpsimd.tensor_tensor(tiles(xc[:, :]), tiles(x_of(n, 0, TILES)), spread(nmean[:, :], TILES),
                                        ALU.add).then_inc(xc_ready, 1)

            def normalise(n):
                pool.wait_ge(ssq_ready, n + 1)
                nc.gpsimd.tensor_tensor(var[:, :], ssq[:, :], inv_d[:, :], ALU.mult).then_inc(var_ready, 1)
                pool.wait_ge(var_ready, 2 * n + 1)
                nc.gpsimd.tensor_tensor(var[:, :], var[:, :], eps[:, :], ALU.add).then_inc(var_ready, 1)
                pool.wait_ge(var_ready, 2 * n + 2)
                nc.gpsimd.tensor_tensor(rstd[:, :], var[:, :], neg_half[:, :], ALU.pow).then_inc(rstd_ready, 1)
                pool.wait_ge(rstd_ready, n + 1)
                nc.gpsimd.tensor_tensor(tiles(xc[:, :]), tiles(xc[:, :]), spread(rstd[:, :], TILES),
                                        ALU.mult).then_inc(hn_ready, 1)

            def divide(n, half):
                pool.wait_ge(rden_ready, 2 * n + half + 1)
                nc.gpsimd.tensor_tensor(tiles(y[:, half]), num[:, half, :, 0:D], spread(rden[:, half], HT),
                                        ALU.mult).then_inc(y_ready, 1)

            def residual(n, half):
                pool.wait_ge(elu_ready, 2 * n + half + 1)
                wait(pool, stored[half], 16 * n)
                nc.gpsimd.tensor_tensor(res[:, half], ey[:, half], x_of(n, half * HT, (half + 1) * HT),
                                        ALU.add).then_inc(res_ready, 1)

            def prologue():
                nc.gpsimd.memset(ident[:, :], 0.0).then_inc(zeroed, 1)
                nc.gpsimd.memset(ones[:, :], 1.0).then_inc(consts_ready, 1)
                nc.gpsimd.memset(neg_half[:, :], -0.5).then_inc(consts_ready, 1)
                nc.gpsimd.memset(inv_d[:, :], 1.0 / D).then_inc(consts_ready, 1)
                nc.gpsimd.memset(neg_inv_d[:, :], -1.0 / D).then_inc(consts_ready, 1)
                nc.gpsimd.memset(eps[:, :], EPS).then_inc(consts_ready, 1)
                nc.gpsimd.memset(shift_f[:, 0:1], -1.0).then_inc(consts_ready, 1)
                nc.gpsimd.memset(shift_f[:, 1:2], -ALPHA).then_inc(consts_ready, 1)
                nc.gpsimd.memset(shift_f[:, 2:3], FACTOR).then_inc(consts_ready, 1)
                nc.gpsimd.memset(wh[:, :, :, UW:UW + 1], 1.0).then_inc(consts_ready, 1)
                nc.gpsimd.memset(tiny_row[:, :, D:D + 1], TINY * N).then_inc(consts_ready, 1)
                pool.wait_ge(zeroed, 1)
                nc.gpsimd.affine_select(out=ident[:, :], in_=ident[:, :], compare_op=ALU.not_equal, fill=1.0,
                                        base=0, pattern=[[-1, P]], channel_multiplier=1).then_inc(ident_ready, 1)
                pool.wait_ge(consts_ready, CONSTANTS)
                centre(0, 0)
                normalise(0)
                centre(1, 1)
                normalise(1)

            def first(b, prep, prev):
                if prev:
                    divide(b[0] - 1, 1)
                    residual(b[0] - 1, 1)

            def second(b, after, ahead):
                divide(b[0], 0)
                if ahead:
                    centre(ahead[0], 2)
                residual(b[0], 0)
                if ahead:
                    normalise(ahead[0])

            def epilogue():
                divide(BATCHES - 1, 1)
                residual(BATCHES - 1, 1)

            schedule(pool, first, second, prologue, epilogue)

        @block.scalar
        def _(act):
            def square(n):
                act.wait_ge(xc_ready, n + 1)
                nc.scalar.activation(xsq[:, :], xc[:, :], ACT.Square).then_inc(xsq_ready, 1)

            def drain_hT(n, par):
                for half in range(2):
                    act.wait_ge(prep_filled, FILLS * n + half + 1)
                    nc.scalar.activation(hT[:, half * HN:(half + 1) * HN], prep[(par + half) % 2][:, :], ACT.Relu,
                                         accum_out=hsum[:, half:half + 1]).then_inc(prep_drained, 1)
                act.wait_ge(prep_drained, FILLS * n + 2)
                nc.scalar.activation(hsum_wide[:, :], ones[:, :], ACT.Identity, scale=hsum[:, 0:1],
                                     bias=hsum[:, 1:2]).then_inc(hsum_ready, 1)

            def drain_wh(n, par):
                for i, (t0, t1) in enumerate(WH_FILLS):
                    f = 2 + i
                    act.wait_ge(prep_filled, FILLS * n + f + 1)
                    src = prep[(par + f) % 2][:, 0:(t1 - t0) * UW].rearrange("p (t c) -> p t c", c=UW)
                    done = nc.scalar.activation(wh[:, par, t0:t1, 0:UW], src, ACT.Copy)
                    if t1 == TILES:
                        wait(act, num_copied, 4 * (n - 1))
                        o = (t1 - t0) * UW + 2
                        done = nc.scalar.activation(tiny_row[:, par, 0:D], prep[(par + f) % 2][:, o:o + D], ACT.Copy,
                                                    scale=TINY)
                    done.then_inc(prep_drained, 1)

            def exps(n, par):
                act.wait_ge(prep_drained, FILLS * n + FILLS - 2)
                act.wait_ge(shift_ready, n + 1)
                nc.scalar.activation(b_col[:, par], wh[:, par, :, 1], ACT.Exp, bias=shift[:, 0:1])
                nc.scalar.activation(d_col[:, par], wh[:, par, :, 1], ACT.Exp, bias=shift[:, 1:2], scale=ALPHA)
                for half in range(2):
                    f = FILLS - 2 + half
                    act.wait_ge(prep_filled, FILLS * n + f + 1)
                    done = nc.scalar.activation(g_row[:, par, half * HN:(half + 1) * HN], prep[(par + f) % 2][:, :],
                                                ACT.Exp, bias=shift[:, 2:3], scale=FACTOR)
                    done.then_inc(prep_drained, 1)
                act.wait_ge(prep_drained, FILLS * (n + 1))
                nc.scalar.activation(ones[0:1, 0:1], ones[0:1, 0:1], ACT.Copy).then_inc(gbd_ready, 1)

            def exp_of_negative_part(n, half):
                act.wait_ge(y_ready, 2 * n + half + 1)
                nc.scalar.activation(ey[:, half], y[:, half], ACT.Relu, scale=-1.0).then_inc(neg_ready, 1)
                act.wait_ge(neg_ready, 2 * n + half + 1)
                nc.scalar.activation(ey[:, half], ey[:, half], ACT.Exp, scale=-1.0).then_inc(ey_ready, 1)

            def prologue():
                act.wait_ge(consts_ready, CONSTANTS)
                square(0)
                drain_hT(0, 0)
                square(1)
                drain_wh(0, 0)
                exps(0, 0)

            def first(b, prep, prev):
                if prep:
                    drain_hT(*next_of(b))
                if prev:
                    exp_of_negative_part(b[0] - 1, 1)
                if prep:
                    drain_wh(*next_of(b))
                    exps(*next_of(b))

            def second(b, after, ahead):
                exp_of_negative_part(b[0], 0)
                if ahead:
                    square(ahead[0])

            def epilogue():
                exp_of_negative_part(BATCHES - 1, 1)

            schedule(act, first, second, prologue, epilogue)

        @block.vector
        def _(dve):
            def row_sums(n, x_sem):
                dve.wait_ge(x_loaded[x_sem], 16)
                nc.vector.tensor_reduce(rsum[:, :], tiles(x_of(n, 0, TILES)), AX.X, ALU.add).then_inc(rsum_ready, 1)

            def square_sums(n):
                dve.wait_ge(xsq_ready, n + 1)
                nc.vector.tensor_reduce(ssq[:, :], tiles(xsq[:, :]), AX.X, ALU.add).then_inc(ssq_ready, 1)

            def score_maxima(n, par):
                dve.wait_ge(prep_drained, FILLS * n + FILLS - 2)
                nc.vector.tensor_reduce(smax[:, bass.ds(n, 1)], wh[:, par, :, 0:2], AX.XY, ALU.max,
                                        apply_absolute_value=True)
                nc.vector.tensor_reduce(sjmax[:, :], wh[:, par, :, 1], AX.X, ALU.max).then_inc(sjmax_ready, 1)

            def score_shift(n, par):
                dve.wait_ge(m_filled, n + 1)
                nc.vector.tensor_reduce(m_all[:, :], prep[(par + FILLS - 1) % 2][:, 0:P], AX.X, ALU.max
                                        ).then_inc(m_ready, 1)
                dve.wait_ge(m_ready, n + 1)
                wait(dve, gbd_ready, n)
                nc.vector.tensor_scalar(shift[:, :], shift_f[:, :], m_all[:, 0:1], None, ALU.mult).then_inc(shift_ready, 1)

            def edge_weights(b, half, g):
                n, par, _ = b
                q = 8 * n + 4 * half + g
                if g == 0:
                    dve.wait_ge(gbd_ready, n + 1)
                for jt in (2 * g, 2 * g + 1):
                    e = nc.vector.tensor_scalar(weights[:, half, jt], g_row[:, par, half * HN:(half + 1) * HN],
                                                b_col[:, par, jt:jt + 1], d_col[:, par, jt:jt + 1], ALU.mult, ALU.max)
                e.then_inc(e_ready, 1)
                dve.wait_ge(e_ready, q + 1)
                dve.wait_ge(adjT_ready, q + 1)
                pair = weights[:, half, 2 * g:2 * g + 2]
                nc.vector.scalar_tensor_tensor(pair, adjT[g % 2].bitcast(I32)[:, :, :], 0.0, pair,
                                               ALU.is_gt, ALU.mult).then_inc(masked, 1)

            def copy_pair(b, half, pair):
                n, par, _ = b
                dve.wait_ge(num_summed, 4 * n + 2 * half + pair + 1)
                if pair == 0:
                    wait(dve, y_ready, 2 * n)
                src = nump[pair][:, 0:2 * NW].rearrange("p (t c) -> p t c", c=NW)
                nc.vector.tensor_tensor(num[:, half, 2 * pair:2 * pair + 2], src,
                                        tiny_row[:, par:par + 1, :].to_broadcast([P, 2, NW]),
                                        ALU.add).then_inc(num_copied, 1)
                if pair == 1:
                    dve.wait_ge(num_copied, 4 * n + 2 * half + 2)
                    nc.vector.reciprocal(rden[:, half], num[:, half, :, D]).then_inc(rden_ready, 1)

            def elu(n, half):
                dve.wait_ge(ey_ready, 2 * n + half + 1)
                nc.vector.scalar_tensor_tensor(ey[:, half], ey[:, half], -1.0, y[:, half],
                                               ALU.add, ALU.max).then_inc(elu_ready, 1)

            def prologue():
                row_sums(0, 0)
                dve.wait_ge(setup_products, 1)
                nc.vector.tensor_copy(u[:, 2:UW], nump[0][:, 0:D]).then_inc(u_ready, 1)
                nc.vector.tensor_copy(u[:, 0:2], nump[1][:, 0:2]).then_inc(u_ready, 1)
                dve.wait_ge(consts_ready, CONSTANTS)
                dve.wait_ge(u_ready, 2)
                nc.vector.tensor_scalar(u1_wide[:, :], ones[:, :], u[:, 0:1], None, ALU.mult).then_inc(u_ready, 1)
                square_sums(0)
                row_sums(1, 1)
                score_maxima(0, 0)
                score_shift(0, 0)
                square_sums(1)
                for g in range(4):
                    edge_weights(fixed(0), 0, g)

            def first(b, prep, prev):
                edge_weights(b, 1, 0)
                edge_weights(b, 1, 1)
                if prev:
                    elu(b[0] - 1, 1)
                if prep:
                    score_maxima(*next_of(b))
                edge_weights(b, 1, 2)
                copy_pair(b, 0, 0)
                if prep:
                    score_shift(*next_of(b))
                edge_weights(b, 1, 3)
                copy_pair(b, 0, 1)

            def second(b, after, ahead):
                if after:
                    edge_weights(after, 0, 0)
                if ahead:
                    row_sums(ahead[0], 2)
                if after:
                    edge_weights(after, 0, 1)
                elu(b[0], 0)
                if after:
                    edge_weights(after, 0, 2)
                copy_pair(b, 1, 0)
                if ahead:
                    square_sums(ahead[0])
                if after:
                    edge_weights(after, 0, 3)
                copy_pair(b, 1, 1)

            def epilogue():
                elu(BATCHES - 1, 1)

            schedule(dve, first, second, prologue, epilogue)

        @block.tensor
        def _(pe):
            def open_fill(n, f):
                wait(pe, prep_drained, FILLS * n + f - 1)

            def fill_hT(n, par, half):
                if half == 0:
                    pe.wait_ge(hn_ready, n + 1)
                open_fill(n, half)
                for t in range(HT):
                    last = nc.tensor.transpose(prep[(par + half) % 2][:, t * P:(t + 1) * P],
                                               xc[:, (half * HT + t) * D:(half * HT + t + 1) * D], ident[:, :])
                last.then_inc(prep_filled, 1)

            def fill_wh(n, par, i):
                f = 2 + i
                t0, t1 = WH_FILLS[i]
                open_fill(n, f)
                pe.wait_ge(prep_drained, FILLS * n + 2)
                bank = prep[(par + f) % 2]
                for t in range(t0, t1):
                    last = nc.tensor.matmul(bank[:, (t - t0) * UW:(t - t0 + 1) * UW], hT[:, t * P:(t + 1) * P], u[:, :],
                                            start=True, stop=True)
                if t1 == TILES:
                    pe.wait_ge(hsum_ready, n + 1)
                    last = nc.tensor.matmul(bank[:, (t1 - t0) * UW:(t1 - t0 + 1) * UW], hsum_wide[:, :], u[:, :],
                                            start=True, stop=True)
                last.then_inc(prep_filled, 1)

            def fill_m(n, par):
                pe.wait_ge(sjmax_ready, n + 1)
                nc.tensor.transpose(prep[(par + FILLS - 1) % 2][:, 0:P], sjmax[:, 0:1].to_broadcast([P, P]),
                                    ident[:, :]).then_inc(m_filled, 1)

            def fill_si(n, par, half):
                f = FILLS - 2 + half
                open_fill(n, f)
                if half:
                    pe.wait_ge(m_ready, n + 1)
                nc.tensor.matmul(prep[(par + f) % 2][:, :], u1_wide[:, :], hT[:, half * HN:(half + 1) * HN],
                                 start=True, stop=True).then_inc(prep_filled, 1)

            def transpose_group(b, half, g):
                n, par, rnd = b
                q = 8 * n + 4 * half + g
                slot = 2 * par + half
                if g == 0:
                    pe.wait_ge(adj_loaded[slot], 16 * (rnd + 1))
                wait(pe, masked, q - 1)
                for jj in range(2):
                    jt = 2 * g + jj
                    for t in range(HT):
                        last = nc.tensor.transpose(adjT[g % 2][:, jj, t * P:(t + 1) * P],
                                                   adj_rows.bitcast(FP32)[:, slot, t, jt * P:(jt + 1) * P], ident[:, :])
                last.then_inc(adjT_ready, 1)

            def sum_tile(b, half, g):
                n, par, _ = b
                if g == 0:
                    pe.wait_ge(masked, 8 * n + 4 * half + 4)
                if g % 2 == 0:
                    wait(pe, num_copied, 4 * n + 2 * half + g // 2 - 1)
                dst = nump[g // 2][:, (g % 2) * NW:(g % 2 + 1) * NW]
                for jt in range(TILES):
                    last = nc.tensor.matmul(dst, weights[:, half, jt, g * P:(g + 1) * P], wh[:, par, jt, 2:2 + NW],
                                            start=jt == 0, stop=jt == TILES - 1)
                if g % 2:
                    last.then_inc(num_summed, 1)

            def prologue():
                pe.wait_ge(weights_loaded, 32)
                pe.wait_ge(ident_ready, 1)
                nc.tensor.transpose(nump[0][:, 0:D], w_rows[:, :], ident[:, :])
                nc.tensor.matmul(nump[1][:, 0:2], w_rows[:, :], a_cols[:, :], start=True, stop=True
                                 ).then_inc(setup_products, 1)
                fill_hT(0, 0, 0)
                fill_hT(0, 0, 1)
                pe.wait_ge(u_ready, 3)
                for i in range(len(WH_FILLS)):
                    fill_wh(0, 0, i)
                fill_m(0, 0)
                fill_si(0, 0, 0)
                fill_si(0, 0, 1)
                for g in range(4):
                    transpose_group(fixed(0), 0, g)

            def first(b, prep, prev):
                m = next_of(b)
                transpose_group(b, 1, 0)
                if prep:
                    fill_hT(*m, 0)
                    fill_hT(*m, 1)
                sum_tile(b, 0, 0)
                transpose_group(b, 1, 1)
                if prep:
                    fill_wh(*m, 0)
                    fill_wh(*m, 1)
                sum_tile(b, 0, 1)
                transpose_group(b, 1, 2)
                if prep:
                    fill_wh(*m, 2)
                sum_tile(b, 0, 2)
                transpose_group(b, 1, 3)
                if prep:
                    fill_m(*m)
                    fill_si(*m, 0)
                sum_tile(b, 0, 3)
                if prep:
                    fill_si(*m, 1)

            def second(b, after, ahead):
                for g in range(4):
                    if after:
                        transpose_group(after, 0, g)
                    sum_tile(b, 1, g)

            schedule(pe, first, second, prologue)


def kernel(x, adj, L0_gnn_W, L0_gnn_a):
    import numpy as np
    import concourse.bacc as bacc
    from concourse.bass_utils import run_bass_kernel_spmd

    nc = bacc.Bacc("TRN2", target_bir_lowering=False, num_devices=1)
    arrays, args = {}, []
    for name, value in (("x", x), ("adj", adj), ("w", L0_gnn_W), ("a", L0_gnn_a)):
        value = np.ascontiguousarray(value)
        arrays[f"in_{name}"] = value
        args.append(nc.dram_tensor(f"in_{name}", value.shape, mybir.dt.from_np(value.dtype), kind="ExternalInput").ap())
    args.append(nc.dram_tensor("out", x.shape, FP32, kind="ExternalOutput").ap())
    graph_attention_kernel(nc, *args)
    r = run_bass_kernel_spmd(nc, [arrays], core_ids=[0])
    return r.results[0]["out"]
```

```python
import concourse.bass as bass
from concourse import mybir
from contextlib import ExitStack

FP32 = mybir.dt.float32
BF16 = mybir.dt.bfloat16
I32 = mybir.dt.int32
ALU = mybir.AluOpType
ACT = mybir.ActivationFunctionType
AX = mybir.AxisListType


def graph_attention_kernel(nc, x, adj, w, a, out):
    BATCHES, N, D = x.shape
    P = 128
    TILES = N // P
    HT = TILES // 2
    HN = N // 2
    UW = D + 2
    NW = D + 1
    ALPHA = 0.2
    EPS = 1e-5
    CONSTANTS = 7
    LARGE = 2.0 ** 90
    TINY = 2.0 ** -100
    SAFE_SCORE = 30.0
    LOOPS = (BATCHES - 2) // 2
    FACTOR = 1.0 - ALPHA
    WH_FILLS = ((0, 3), (3, 6), (6, 8))
    FILLS = 4 + len(WH_FILLS)

    x_t = x.rearrange("b (t p) d -> b p t d", p=P)
    out_t = out.rearrange("b (t p) d -> b p t d", p=P)
    adj_t = adj.rearrange("b (t p) j -> b p t j", p=P)

    ctx = ExitStack()
    with ctx:
        def sb(name, shape, dt=FP32):
            return ctx.enter_context(nc.sbuf_tensor(name, shape, dt))

        def sem(name):
            return ctx.enter_context(nc.semaphore(name))

        adj_rows = sb("adj_rows", [P, 4, HT, N], I32)
        weights = sb("weights", [P, 2, TILES, HN])
        xs = sb("xs", [P, BATCHES, TILES * D])
        xn = sb("xn", [P, TILES * D])
        stats = sb("stats", [P, TILES, 6])
        mean_var = sb("mean_var", [P, TILES, 2])
        hT = sb("hT", [P, N])
        wh = sb("wh", [P, TILES, D + 3])
        v = sb("v", [P, 2, TILES, NW])
        edges = sb("edges", [P, 2, HT, N], BF16)
        g_row = sb("g_row", [P, 2, N])
        b_col = sb("b_col", [P, TILES])
        q_col = sb("q_col", [P, 2, TILES])
        tiny_row = sb("tiny_row", [P, 2, NW])
        num = sb("num", [P, 2, HT, NW])
        rden = sb("rden", [P, 2, HT])
        y = sb("y", [P, 2, HT * D])
        ey = sb("ey", [P, 2, HT * D])
        res = sb("res", [P, 2, HT * D])
        ident = sb("ident", [P, P])
        ident_bf = sb("ident_bf", [P, P], BF16)
        ones = sb("ones", [P, P])
        w_rows = sb("w_rows", [P, D])
        a_cols = sb("a_cols", [P, 2])
        u = sb("u", [P, UW])
        hsum = sb("hsum", [P, 2])
        hsum_wide = sb("hsum_wide", [P, P])
        var = sb("var", [P, TILES])
        rstd = sb("rstd", [P, TILES])
        neg_half = sb("neg_half", [P, TILES])
        eps = sb("eps", [P, TILES])
        sjmax = sb("sjmax", [P, 1])
        m_all = sb("m_all", [P, 1])
        shift = sb("shift", [P, 2])
        shift_f = sb("shift_f", [P, 2])
        smax = sb("smax", [P, BATCHES])

        adjT = [ctx.enter_context(nc.psum_tensor(f"adjT{i}", [P, 2, HN], BF16)) for i in range(4)]
        nump = [ctx.enter_context(nc.psum_tensor(f"nump{i}", [P, 512], FP32)) for i in range(2)]
        prep = [ctx.enter_context(nc.psum_tensor(f"prep{i}", [P, 512], FP32)) for i in range(2)]

        def dma_sems(name, n):
            return [sem(f"{name}{i}") for i in range(n)]

        zeroed, ident_ready, consts_ready = sem("zeroed"), sem("ident_ready"), sem("consts_ready")
        setup_products = sem("setup_products")
        u_ready = sem("u_ready")
        adj_loaded = dma_sems("adj_loaded", 4)
        x_loaded = dma_sems("x_loaded", 3)
        stats_ready, mean_var_ready = sem("stats_ready"), sem("mean_var_ready")
        var_ready, rstd_ready = sem("var_ready"), sem("rstd_ready")
        xn_ready = sem("xn_ready")
        prep_filled = sem("prep_filled")
        prep_drained = sem("prep_drained")
        hsum_ready = sem("hsum_ready")
        sjmax_ready, m_ready, shift_ready = sem("sjmax_ready"), sem("m_ready"), sem("shift_ready")
        m_filled = sem("m_filled")
        cols_ready = sem("cols_ready")
        v_ready = sem("v_ready")
        edges_ready = sem("edges_ready")
        adjT_ready = sem("adjT_ready")
        weighted = sem("weighted")
        num_summed = sem("num_summed")
        num_copied = sem("num_copied")
        rden_ready, y_ready, neg_ready = sem("rden_ready"), sem("y_ready"), sem("neg_ready")
        ey_ready, elu_ready, res_ready = sem("ey_ready"), sem("elu_ready"), sem("res_ready")
        small_moves = dma_sems("small_moves", 2)

        block = ctx.enter_context(nc.Block())

        def fixed(n):
            return n, n % 2, n // 2

        def looped(k, c):
            return 2 * k + c, c % 2, k + c // 2

        def wait(eng, semaphore, count):
            if not isinstance(count, int) or count > 0:
                eng.wait_ge(semaphore, count)

        def schedule(eng, first, second, prologue, epilogue=None):
            prologue()
            first(fixed(0), fixed(1), prep=True, prev=False)
            with eng.Fori(0, LOOPS) as k:
                for c in range(2):
                    second(looped(k, c), looped(k, c + 1), looped(k, c + 2))
                    first(looped(k, c + 1), looped(k, c + 2), prep=True, prev=True)
            second(fixed(BATCHES - 2), fixed(BATCHES - 1), None)
            first(fixed(BATCHES - 1), None, prep=False, prev=True)
            second(fixed(BATCHES - 1), None, None)
            if epilogue:
                epilogue()

        def x_of(n, t0, t1):
            return xs[:, bass.ds(n, 1), t0 * D:t1 * D].rearrange("p o f -> p (o f)")

        def tiles(ap):
            return ap.rearrange("p (t d) -> p t d", d=D)

        def spread(ap, n):
            return ap.unsqueeze(2).to_broadcast([P, n, D])

        def next_of(b):
            return b[0] + 1, 1 - b[1]

        @block.sync
        def _(sp):
            def load_x(n0, n1, s):
                sp.dma_start(xs[:, n0:n1, :].rearrange("p b (t d) -> p b t d", d=D),
                             x_t[n0:n1].rearrange("b p t d -> p b t d")).then_inc(x_loaded[s], 16)

            def load_adj(n, par, half):
                src = adj_t[bass.ds(n, 1), :, half * HT:(half + 1) * HT, :].rearrange("o p t j -> p (o t) j")
                sp.dma_start(adj_rows[:, 2 * par + half], src).then_inc(adj_loaded[2 * par + half], 16)

            def store(n, half):
                sp.wait_ge(res_ready, 2 * n + half + 1)
                dst = out_t[bass.ds(n, 1), :, half * HT:(half + 1) * HT, :].rearrange("o p t d -> p (o t) d")
                sp.dma_start(dst, tiles(res[:, half])).then_inc(small_moves[half], 16)

            def prologue():
                load_x(0, 1, 0)
                sp.dma_start(w_rows[:, :], w).then_inc(small_moves[0], 16)
                with nc.allow_non_contiguous_dma(reason="a is 256 numbers, turned into two columns"):
                    sp.dma_start(a_cols[:, :], a.rearrange("o (c p) -> p (o c)", p=P)).then_inc(small_moves[1], 16)
                load_adj(0, 0, 0)
                load_x(1, 2, 1)
                load_adj(0, 0, 1)
                load_adj(1, 1, 0)
                load_x(2, BATCHES, 2)
                load_adj(1, 1, 1)

            def first(b, after, prep, prev):
                if prev:
                    store(b[0] - 1, 1)

            def second(b, after, ahead):
                if ahead:
                    for half in range(2):
                        sp.wait_ge(edges_ready, 8 * b[0] + 4 * half + 4)
                        load_adj(ahead[0], ahead[1], half)
                store(b[0], 0)

            def epilogue():
                store(BATCHES - 1, 1)
                for half in range(2):
                    sp.wait_ge(small_moves[half], 16 * (BATCHES + 1))

            schedule(sp, first, second, prologue, epilogue)

        @block.gpsimd
        def _(pool):
            def constants():
                pool.wait_ge(consts_ready, CONSTANTS)

            def reciprocal_deviation(n):
                pool.wait_ge(mean_var_ready, n + 1)
                nc.gpsimd.tensor_tensor(var[:, :], mean_var[:, :, 1], eps[:, :], ALU.add).then_inc(var_ready, 1)
                pool.wait_ge(var_ready, n + 1)
                nc.gpsimd.tensor_tensor(rstd[:, :], var[:, :], neg_half[:, :], ALU.pow).then_inc(rstd_ready, 1)

            def scale_rows(n, par):
                pool.wait_ge(cols_ready, n + 1)
                nc.gpsimd.tensor_tensor(v[:, par], wh[:, :, 2:2 + NW], b_col[:, :].unsqueeze(2).to_broadcast([P, TILES, NW]),
                                        ALU.mult).then_inc(v_ready, 1)

            def divide(n, half):
                pool.wait_ge(rden_ready, 2 * n + half + 1)
                nc.gpsimd.tensor_tensor(tiles(y[:, half]), num[:, half, :, 0:D], spread(rden[:, half], HT),
                                        ALU.mult).then_inc(y_ready, 1)

            def residual(n, half):
                pool.wait_ge(elu_ready, 2 * n + half + 1)
                pool.wait_ge(small_moves[half], 16 * (n + 1))
                nc.gpsimd.tensor_tensor(res[:, half], ey[:, half], x_of(n, half * HT, (half + 1) * HT),
                                        ALU.add).then_inc(res_ready, 1)

            def prologue():
                nc.gpsimd.memset(ident[:, :], 0.0).then_inc(zeroed, 1)
                nc.gpsimd.memset(ones[:, :], 1.0).then_inc(consts_ready, 1)
                nc.gpsimd.memset(neg_half[:, :], -0.5).then_inc(consts_ready, 1)
                nc.gpsimd.memset(eps[:, :], EPS).then_inc(consts_ready, 1)
                nc.gpsimd.memset(shift_f[:, 0:1], -1.0).then_inc(consts_ready, 1)
                nc.gpsimd.memset(shift_f[:, 1:2], FACTOR).then_inc(consts_ready, 1)
                nc.gpsimd.memset(wh[:, :, UW:UW + 1], 1.0).then_inc(consts_ready, 1)
                nc.gpsimd.memset(tiny_row[:, :, D:D + 1], TINY * N).then_inc(consts_ready, 1)
                pool.wait_ge(zeroed, 1)
                nc.gpsimd.affine_select(out=ident[:, :], in_=ident[:, :], compare_op=ALU.not_equal, fill=1.0,
                                        base=0, pattern=[[-1, P]], channel_multiplier=1).then_inc(ident_ready, 1)
                pool.wait_ge(ident_ready, 1)
                nc.gpsimd.tensor_copy(ident_bf[:, :], ident[:, :]).then_inc(ident_ready, 1)
                pool.wait_ge(consts_ready, CONSTANTS)
                reciprocal_deviation(0)
                reciprocal_deviation(1)
                scale_rows(0, 0)

            def first(b, after, prep, prev):
                if prev:
                    divide(b[0] - 1, 1)
                    residual(b[0] - 1, 1)
                if prep:
                    scale_rows(*next_of(b))

            def second(b, after, ahead):
                divide(b[0], 0)
                if ahead:
                    reciprocal_deviation(ahead[0])
                residual(b[0], 0)

            def epilogue():
                divide(BATCHES - 1, 1)
                residual(BATCHES - 1, 1)

            schedule(pool, first, second, prologue, epilogue)

        @block.scalar
        def _(act):
            def drain_hT(n, par):
                for half in range(2):
                    act.wait_ge(prep_filled, FILLS * n + half + 1)
                    nc.scalar.activation(hT[:, half * HN:(half + 1) * HN], prep[(par + half) % 2][:, :], ACT.Relu,
                                         accum_out=hsum[:, half:half + 1]).then_inc(prep_drained, 1)
                act.wait_ge(prep_drained, FILLS * n + 2)
                nc.scalar.activation(hsum_wide[:, :], ones[:, :], ACT.Identity, scale=hsum[:, 0:1],
                                     bias=hsum[:, 1:2]).then_inc(hsum_ready, 1)

            def drain_wh(n, par):
                for i, (t0, t1) in enumerate(WH_FILLS):
                    f = 2 + i
                    act.wait_ge(prep_filled, FILLS * n + f + 1)
                    src = prep[(par + f) % 2][:, 0:(t1 - t0) * UW].rearrange("p (t c) -> p t c", c=UW)
                    done = nc.scalar.activation(wh[:, t0:t1, 0:UW], src, ACT.Copy)
                    if t1 == TILES:
                        wait(act, num_copied, 4 * (n - 1))
                        o = (t1 - t0) * UW + 2
                        done = nc.scalar.activation(tiny_row[:, par, 0:D], prep[(par + f) % 2][:, o:o + D], ACT.Copy,
                                                    scale=TINY)
                    done.then_inc(prep_drained, 1)

            def exps(n, par):
                act.wait_ge(prep_drained, FILLS * n + FILLS - 2)
                act.wait_ge(shift_ready, n + 1)
                nc.scalar.activation(q_col[:, par], wh[:, :, 1], ACT.Exp, bias=shift[:, 1:2], scale=-FACTOR)
                nc.scalar.activation(b_col[:, :], wh[:, :, 1], ACT.Exp, bias=shift[:, 0:1]).then_inc(cols_ready, 1)
                for half in range(2):
                    f = FILLS - 2 + half
                    act.wait_ge(prep_filled, FILLS * n + f + 1)
                    nc.scalar.activation(g_row[:, par, half * HN:(half + 1) * HN], prep[(par + f) % 2][:, :],
                                         ACT.Exp, bias=shift[:, 1:2], scale=FACTOR).then_inc(prep_drained, 1)

            def mark_edges(b, half, g):
                n, par, rnd = b
                slot = 2 * par + half
                if g == 0:
                    act.wait_ge(adj_loaded[slot], 16 * (rnd + 1))
                    wait(act, adjT_ready, 8 * n + 4 * half - 4)
                cols = slice(2 * g * P, 2 * (g + 1) * P)
                nc.scalar.activation(edges[:, half, :, cols], adj_rows[:, slot, :, cols], ACT.Relu,
                                     scale=LARGE).then_inc(edges_ready, 1)

            def exp_of_negative_part(n, half):
                act.wait_ge(y_ready, 2 * n + half + 1)
                nc.scalar.activation(ey[:, half], y[:, half], ACT.Relu, scale=-1.0).then_inc(neg_ready, 1)
                act.wait_ge(neg_ready, 2 * n + half + 1)
                nc.scalar.activation(ey[:, half], ey[:, half], ACT.Exp, scale=-1.0).then_inc(ey_ready, 1)

            def prologue():
                act.wait_ge(consts_ready, CONSTANTS)
                drain_hT(0, 0)
                for g in range(2):
                    mark_edges(fixed(0), 0, g)
                drain_wh(0, 0)
                for g in range(2, 4):
                    mark_edges(fixed(0), 0, g)
                exps(0, 0)
                for g in range(4):
                    mark_edges(fixed(0), 1, g)

            def first(b, after, prep, prev):
                if prep:
                    drain_hT(*next_of(b))
                if prev:
                    exp_of_negative_part(b[0] - 1, 1)
                if after:
                    mark_edges(after, 0, 0)
                    mark_edges(after, 0, 1)
                if prep:
                    drain_wh(*next_of(b))
                if after:
                    mark_edges(after, 0, 2)
                if prep:
                    exps(*next_of(b))
                if after:
                    mark_edges(after, 0, 3)

            def second(b, after, ahead):
                if after:
                    mark_edges(after, 1, 0)
                exp_of_negative_part(b[0], 0)
                if after:
                    mark_edges(after, 1, 1)
                    mark_edges(after, 1, 2)
                if after:
                    mark_edges(after, 1, 3)

            def epilogue():
                exp_of_negative_part(BATCHES - 1, 1)

            schedule(act, first, second, prologue, epilogue)

        @block.vector
        def _(dve):
            def row_statistics(n, x_sem):
                dve.wait_ge(x_loaded[x_sem], 16)
                for t in range(TILES):
                    last = nc.vector.bn_stats(stats[:, t], x_of(n, t, t + 1))
                last.then_inc(stats_ready, 1)

            def stats_landed(n):
                dve.wait_ge(stats_ready, n + 1)
                wait(dve, rstd_ready, n)

            def aggregate():
                for t in range(TILES):
                    last = nc.vector.bn_aggr(mean_var[:, t], stats[:, t])
                last.then_inc(mean_var_ready, 1)

            def normalise(n):
                wait(dve, prep_filled, FILLS * (n - 1) + 2)
                dve.wait_ge(rstd_ready, n + 1)
                for t in range(TILES):
                    done = nc.vector.tensor_scalar(xn[:, t * D:(t + 1) * D], x_of(n, t, t + 1), mean_var[:, t, 0:1],
                                                   rstd[:, t:t + 1], ALU.subtract, ALU.mult)
                    if t % HT == HT - 1:
                        done.then_inc(xn_ready, 1)

            def score_maxima(n, par):
                dve.wait_ge(prep_drained, FILLS * n + FILLS - 2)
                nc.vector.tensor_reduce(smax[:, bass.ds(n, 1)], wh[:, :, 0:2], AX.XY, ALU.max,
                                        apply_absolute_value=True)
                nc.vector.tensor_reduce(sjmax[:, :], wh[:, :, 1], AX.X, ALU.max).then_inc(sjmax_ready, 1)

            def score_shift(n, par):
                dve.wait_ge(m_filled, n + 1)
                nc.vector.tensor_reduce(m_all[:, :], prep[(par + FILLS - 1) % 2][:, 0:P], AX.X, ALU.max
                                        ).then_inc(m_ready, 1)
                dve.wait_ge(m_ready, n + 1)
                wait(dve, prep_drained, FILLS * n)
                nc.vector.tensor_scalar(shift[:, :], shift_f[:, :], m_all[:, 0:1], None, ALU.mult).then_inc(shift_ready, 1)

            def edge_weights(b, half, g):
                n, par, _ = b
                q = 8 * n + 4 * half + g
                if g == 0:
                    dve.wait_ge(prep_drained, FILLS * n + FILLS - 1 + half)
                dve.wait_ge(adjT_ready, q + 1)
                for jj in range(2):
                    jt = 2 * g + jj
                    done = nc.vector.scalar_tensor_tensor(
                        weights[:, half, jt], g_row[:, par, half * HN:(half + 1) * HN], q_col[:, par, jt:jt + 1],
                        adjT[g][:, jj], ALU.max, ALU.min)
                done.then_inc(weighted, 1)

            def copy_pair(b, half, pair):
                n, par, _ = b
                dve.wait_ge(num_summed, 4 * n + 2 * half + pair + 1)
                if pair == 0:
                    wait(dve, y_ready, 2 * n + half)
                src = nump[pair][:, 0:2 * NW].rearrange("p (t c) -> p t c", c=NW)
                nc.vector.tensor_tensor(num[:, half, 2 * pair:2 * pair + 2], src,
                                        tiny_row[:, par:par + 1, :].to_broadcast([P, 2, NW]),
                                        ALU.add).then_inc(num_copied, 1)
                if pair == 1:
                    dve.wait_ge(num_copied, 4 * n + 2 * half + 2)
                    nc.vector.reciprocal(rden[:, half], num[:, half, :, D]).then_inc(rden_ready, 1)

            def elu(n, half):
                dve.wait_ge(ey_ready, 2 * n + half + 1)
                nc.vector.scalar_tensor_tensor(ey[:, half], ey[:, half], -1.0, y[:, half],
                                               ALU.add, ALU.max).then_inc(elu_ready, 1)

            def prologue():
                row_statistics(0, 0)
                stats_landed(0)
                aggregate()
                dve.wait_ge(setup_products, 1)
                nc.vector.tensor_copy(u[:, 2:UW], nump[0][:, 0:D]).then_inc(u_ready, 1)
                nc.vector.tensor_copy(u[:, 0:2], nump[1][:, 0:2]).then_inc(u_ready, 1)
                normalise(0)
                row_statistics(1, 1)
                stats_landed(1)
                aggregate()
                score_maxima(0, 0)
                score_shift(0, 0)
                normalise(1)
                for g in range(4):
                    edge_weights(fixed(0), 0, g)

            def first(b, after, prep, prev):
                edge_weights(b, 1, 0)
                edge_weights(b, 1, 1)
                if prev:
                    elu(b[0] - 1, 1)
                if prep:
                    score_maxima(*next_of(b))
                edge_weights(b, 1, 2)
                copy_pair(b, 0, 0)
                if prep:
                    score_shift(*next_of(b))
                edge_weights(b, 1, 3)
                copy_pair(b, 0, 1)

            def second(b, after, ahead):
                if ahead:
                    row_statistics(ahead[0], 2)
                    stats_landed(ahead[0])
                if after:
                    edge_weights(after, 0, 0)
                if ahead:
                    aggregate()
                if after:
                    edge_weights(after, 0, 1)
                elu(b[0], 0)
                if after:
                    edge_weights(after, 0, 2)
                if ahead:
                    normalise(ahead[0])
                copy_pair(b, 1, 0)
                if after:
                    edge_weights(after, 0, 3)
                copy_pair(b, 1, 1)

            def epilogue():
                elu(BATCHES - 1, 1)

            schedule(dve, first, second, prologue, epilogue)

        @block.tensor
        def _(pe):
            def open_fill(n, f):
                wait(pe, prep_drained, FILLS * n + f - 1)

            def fill_hT(n, par, half):
                pe.wait_ge(xn_ready, 2 * n + half + 1)
                open_fill(n, half)
                for t in range(HT):
                    last = nc.tensor.transpose(prep[(par + half) % 2][:, t * P:(t + 1) * P],
                                               xn[:, (half * HT + t) * D:(half * HT + t + 1) * D], ident[:, :])
                last.then_inc(prep_filled, 1)

            def fill_wh(n, par, i):
                f = 2 + i
                t0, t1 = WH_FILLS[i]
                open_fill(n, f)
                pe.wait_ge(prep_drained, FILLS * n + 2)
                bank = prep[(par + f) % 2]
                for t in range(t0, t1):
                    last = nc.tensor.matmul(bank[:, (t - t0) * UW:(t - t0 + 1) * UW], hT[:, t * P:(t + 1) * P], u[:, :],
                                            start=True, stop=True)
                if t1 == TILES:
                    pe.wait_ge(hsum_ready, n + 1)
                    last = nc.tensor.matmul(bank[:, (t1 - t0) * UW:(t1 - t0 + 1) * UW], hsum_wide[:, :], u[:, :],
                                            start=True, stop=True)
                last.then_inc(prep_filled, 1)

            def fill_m(n, par):
                pe.wait_ge(sjmax_ready, n + 1)
                nc.tensor.transpose(prep[(par + FILLS - 1) % 2][:, 0:P], sjmax[:, 0:1].to_broadcast([P, P]),
                                    ident[:, :]).then_inc(m_filled, 1)

            def fill_si(n, par, half):
                f = FILLS - 2 + half
                open_fill(n, f)
                if half:
                    pe.wait_ge(m_ready, n + 1)
                for t in range(HT):
                    last = nc.tensor.transpose(prep[(par + f) % 2][:, t * P:(t + 1) * P],
                                               wh[:, half * HT + t, 0:1].to_broadcast([P, P]), ident[:, :])
                last.then_inc(prep_filled, 1)

            def transpose_group(b, half, g):
                q = 8 * b[0] + 4 * half + g
                pe.wait_ge(edges_ready, q + 1)
                wait(pe, weighted, q - 3)
                for jj in range(2):
                    jt = 2 * g + jj
                    for t in range(HT):
                        last = nc.tensor.transpose(adjT[g][:, jj, t * P:(t + 1) * P],
                                                   edges[:, half, t, jt * P:(jt + 1) * P], ident_bf[:, :])
                last.then_inc(adjT_ready, 1)

            def sum_tile(b, half, g):
                n, par, _ = b
                if g == 0:
                    pe.wait_ge(weighted, 8 * n + 4 * half + 4)
                    pe.wait_ge(v_ready, n + 1)
                if g % 2 == 0:
                    wait(pe, num_copied, 4 * n + 2 * half + g // 2 - 1)
                dst = nump[g // 2][:, (g % 2) * NW:(g % 2 + 1) * NW]
                for jt in range(TILES):
                    last = nc.tensor.matmul(dst, weights[:, half, jt, g * P:(g + 1) * P], v[:, par, jt],
                                            start=jt == 0, stop=jt == TILES - 1)
                if g % 2:
                    last.then_inc(num_summed, 1)

            def prologue():
                pe.wait_ge(small_moves[0], 16)
                pe.wait_ge(small_moves[1], 16)
                pe.wait_ge(ident_ready, 2)
                nc.tensor.transpose(nump[0][:, 0:D], w_rows[:, :], ident[:, :])
                nc.tensor.matmul(nump[1][:, 0:2], w_rows[:, :], a_cols[:, :], start=True, stop=True
                                 ).then_inc(setup_products, 1)
                fill_hT(0, 0, 0)
                fill_hT(0, 0, 1)
                pe.wait_ge(u_ready, 2)
                for i in range(len(WH_FILLS)):
                    fill_wh(0, 0, i)
                transpose_group(fixed(0), 0, 0)
                transpose_group(fixed(0), 0, 1)
                fill_m(0, 0)
                fill_si(0, 0, 0)
                fill_si(0, 0, 1)
                transpose_group(fixed(0), 0, 2)
                transpose_group(fixed(0), 0, 3)

            def first(b, after, prep, prev):
                m = next_of(b)
                transpose_group(b, 1, 0)
                if prep:
                    fill_hT(*m, 0)
                    fill_hT(*m, 1)
                sum_tile(b, 0, 0)
                transpose_group(b, 1, 1)
                if prep:
                    fill_wh(*m, 0)
                    fill_wh(*m, 1)
                sum_tile(b, 0, 1)
                transpose_group(b, 1, 2)
                if prep:
                    fill_wh(*m, 2)
                sum_tile(b, 0, 2)
                transpose_group(b, 1, 3)
                if prep:
                    fill_m(*m)
                    fill_si(*m, 0)
                sum_tile(b, 0, 3)
                if prep:
                    fill_si(*m, 1)

            def second(b, after, ahead):
                for g in range(4):
                    if after:
                        transpose_group(after, 0, g)
                    sum_tile(b, 1, g)

            schedule(pe, first, second, prologue)


def kernel(x, adj, L0_gnn_W, L0_gnn_a):
    import numpy as np
    import concourse.bacc as bacc
    from concourse.bass_utils import run_bass_kernel_spmd

    nc = bacc.Bacc("TRN2", target_bir_lowering=False, num_devices=1)
    arrays, args = {}, []
    for name, value in (("x", x), ("adj", adj), ("w", L0_gnn_W), ("a", L0_gnn_a)):
        value = np.ascontiguousarray(value)
        arrays[f"in_{name}"] = value
        args.append(nc.dram_tensor(f"in_{name}", value.shape, mybir.dt.from_np(value.dtype), kind="ExternalInput").ap())
    args.append(nc.dram_tensor("out", x.shape, FP32, kind="ExternalOutput").ap())
    graph_attention_kernel(nc, *args)
    r = run_bass_kernel_spmd(nc, [arrays], core_ids=[0])
    return r.results[0]["out"]
```

```python
import concourse.bass as bass
from concourse import mybir
from contextlib import ExitStack

FP32 = mybir.dt.float32
BF16 = mybir.dt.bfloat16
I32 = mybir.dt.int32
ALU = mybir.AluOpType
ACT = mybir.ActivationFunctionType
AX = mybir.AxisListType


def graph_attention_kernel(nc, x, adj, w, a, out):
    BATCHES, N, D = x.shape
    P = 128
    TILES = N // P
    HT = TILES // 2
    HN = N // 2
    UW = D + 2
    NW = D + 1
    ALPHA = 0.2
    EPS = 1e-5
    CONSTANTS = 7
    LARGE = 2.0 ** 90
    TINY = 2.0 ** -100
    SAFE_SCORE = 30.0
    LOOPS = (BATCHES - 2) // 2
    FACTOR = 1.0 - ALPHA
    WH_FILLS = ((0, 3), (3, 6), (6, 8))
    NO_EDGE = -9e15
    FILLS = 4 + len(WH_FILLS)

    x_t = x.rearrange("b (t p) d -> b p t d", p=P)
    out_t = out.rearrange("b (t p) d -> b p t d", p=P)
    adj_t = adj.rearrange("b (t p) j -> b p t j", p=P)

    ctx = ExitStack()
    with ctx:
        def sb(name, shape, dt=FP32):
            return ctx.enter_context(nc.sbuf_tensor(name, shape, dt))

        def sem(name):
            return ctx.enter_context(nc.semaphore(name))

        adj_rows = sb("adj_rows", [P, 4, HT, N], I32)
        weights = sb("weights", [P, 2, TILES, HN])
        xs = sb("xs", [P, BATCHES, TILES * D])
        xn = sb("xn", [P, TILES * D])
        stats = sb("stats", [P, TILES, 6])
        mean_var = sb("mean_var", [P, TILES, 2])
        hT = sb("hT", [P, N])
        wh = sb("wh", [P, TILES, D + 3])
        v = sb("v", [P, 2, TILES, NW])
        edges = sb("edges", [P, 2, HT, N], BF16)
        g_row = sb("g_row", [P, 2, N])
        b_col = sb("b_col", [P, TILES])
        q_col = sb("q_col", [P, 2, TILES])
        tiny_row = sb("tiny_row", [P, 2, NW])
        num = sb("num", [P, 2, HT, NW])
        rden = sb("rden", [P, 2, HT])
        y = sb("y", [P, 2, HT * D])
        ey = sb("ey", [P, 2, HT * D])
        res = sb("res", [P, 2, HT * D])
        ident = sb("ident", [P, P])
        ident_bf = sb("ident_bf", [P, P], BF16)
        ones = sb("ones", [P, P])
        w_rows = sb("w_rows", [P, D])
        a_cols = sb("a_cols", [P, 2])
        u = sb("u", [P, UW])
        hsum = sb("hsum", [P, 2])
        hsum_wide = sb("hsum_wide", [P, P])
        var = sb("var", [P, TILES])
        rstd = sb("rstd", [P, TILES])
        neg_half = sb("neg_half", [P, TILES])
        eps = sb("eps", [P, TILES])
        sjmax = sb("sjmax", [P, 1])
        m_all = sb("m_all", [P, 1])
        shift = sb("shift", [P, 2])
        shift_f = sb("shift_f", [P, 2])
        smax = sb("smax", [P, BATCHES])
        smax_all = sb("smax_all", [P, 1])
        unsafe = sb("unsafe", [P, 1], I32)

        adjT = [ctx.enter_context(nc.psum_tensor(f"adjT{i}", [P, 2, HN], BF16)) for i in range(4)]
        nump = [ctx.enter_context(nc.psum_tensor(f"nump{i}", [P, 512], FP32)) for i in range(2)]
        prep = [ctx.enter_context(nc.psum_tensor(f"prep{i}", [P, 512], FP32)) for i in range(2)]

        def dma_sems(name, n):
            return [sem(f"{name}{i}") for i in range(n)]

        zeroed, ident_ready, consts_ready = sem("zeroed"), sem("ident_ready"), sem("consts_ready")
        setup_products = sem("setup_products")
        u_ready = sem("u_ready")
        adj_loaded = dma_sems("adj_loaded", 4)
        adj_head_loaded = sem("adj_head_loaded")
        x_loaded = dma_sems("x_loaded", 4)
        stats_ready, mean_var_ready = sem("stats_ready"), sem("mean_var_ready")
        var_ready, rstd_ready = sem("var_ready"), sem("rstd_ready")
        xn_ready = sem("xn_ready")
        prep_filled = sem("prep_filled")
        prep_drained = sem("prep_drained")
        hsum_ready = sem("hsum_ready")
        sjmax_ready, m_ready, shift_ready = sem("sjmax_ready"), sem("m_ready"), sem("shift_ready")
        m_filled = sem("m_filled")
        cols_ready = sem("cols_ready")
        v_ready = sem("v_ready")
        edges_ready = sem("edges_ready")
        adjT_ready = sem("adjT_ready")
        weighted = sem("weighted")
        num_summed = sem("num_summed")
        num_copied = sem("num_copied")
        rden_ready, y_ready, neg_ready = sem("rden_ready"), sem("y_ready"), sem("neg_ready")
        ey_ready, elu_ready, res_ready = sem("ey_ready"), sem("elu_ready"), sem("res_ready")
        small_moves = dma_sems("small_moves", 2)
        last_stored = dma_sems("last_stored", HT)
        last_summed, last_copied, last_rden = sem("last_summed"), sem("last_copied"), sem("last_rden")
        last_y, last_neg, last_ey = sem("last_y"), sem("last_neg"), sem("last_ey")
        last_elu, last_res = sem("last_elu"), sem("last_res")
        warmed = sem("warmed")

        smax_ready, smax_filled, smax_known = sem("smax_ready"), sem("smax_filled"), sem("smax_known")
        unsafe_ready = sem("unsafe_ready")

        gen_adj = adj_rows[:, 0, 0]
        gen_e = weights[:, 1, 0:2].rearrange("p a i -> p (a i)")
        gen_mask = weights[:, 1, 2:4].rearrange("p a i -> p (a i)")
        gen_off = weights[:, 1, 4:6].rearrange("p a i -> p (a i)")
        gen_p = weights[:, 1, 6:8].rearrange("p a i -> p (a i)")
        gen_pT = weights[:, 0, 0:2].rearrange("p a i -> p (a i)")
        sj_row = g_row[:, 0]
        gen_max = sb("gen_max", [P, 1])
        gen_sum = sb("gen_sum", [P, 1])
        gen_inv = sb("gen_inv", [P, 1])
        gen_scratch = sb("gen_scratch", [P, 1])
        gen_y, gen_ey, gen_res = y[:, 0, 0:D], ey[:, 0, 0:D], res[:, 0, 0:D]
        gen_stats, gen_mean_var, gen_var = sem("gen_stats"), sem("gen_mean_var"), sem("gen_var")
        gen_rstd, gen_xn = sem("gen_rstd"), sem("gen_xn")
        gen_hT_filled, gen_hT = sem("gen_hT_filled"), sem("gen_hT")
        gen_wh_filled, gen_wh = sem("gen_wh_filled"), sem("gen_wh")
        gen_sj_filled, gen_sj = sem("gen_sj_filled"), sem("gen_sj")
        gen_adj_loaded = sem("gen_adj_loaded")
        gen_chain = sem("gen_chain")
        gen_max_ready, gen_p_ready = sem("gen_max_ready"), sem("gen_p_ready")
        gen_pT_filled, gen_pT_ready = sem("gen_pT_filled"), sem("gen_pT_ready")
        gen_summed, gen_inv_ready, gen_y_ready = sem("gen_summed"), sem("gen_inv_ready"), sem("gen_y_ready")
        gen_neg, gen_ey_ready, gen_elu = sem("gen_neg"), sem("gen_ey_ready"), sem("gen_elu")
        gen_res_ready = sem("gen_res_ready")
        gen_off_added = sem("gen_off_added")
        CHAIN = 5

        block = ctx.enter_context(nc.Block())

        def fixed(n):
            return n, n % 2, n // 2

        def looped(k, c):
            return 2 * k + c, c % 2, k + c // 2

        def wait(eng, semaphore, count):
            if not isinstance(count, int) or count > 0:
                eng.wait_ge(semaphore, count)

        def general_path(eng, batch, tile, end=None):
            eng.wait_ge(unsafe_ready, 1)
            chosen = eng.value_load(unsafe[0:1, 0:1], min_val=0, max_val=1)
            with eng.If(chosen):
                with eng.Fori(0, BATCHES) as n:
                    if batch:
                        batch(n)
                    for t in range(TILES):
                        if tile:
                            tile(n, TILES * n + t, t)
                if end:
                    end()

        def schedule(eng, first, second, prologue, epilogue=None, after_loop=None, after_preparation=None):
            prologue()
            first(fixed(0), fixed(1), prep=True, prev=False)
            with eng.Fori(0, LOOPS) as k:
                for c in range(2):
                    second(looped(k, c), looped(k, c + 1), looped(k, c + 2))
                    first(looped(k, c + 1), looped(k, c + 2), prep=True, prev=True)
            if after_loop:
                after_loop()
            second(fixed(BATCHES - 2), fixed(BATCHES - 1), None)
            if after_preparation:
                after_preparation()
            first(fixed(BATCHES - 1), None, prep=False, prev=True)
            second(fixed(BATCHES - 1), None, None)
            if epilogue:
                epilogue()

        def x_of(n, t0, t1):
            return xs[:, bass.ds(n, 1), t0 * D:t1 * D].rearrange("p o f -> p (o f)")

        def tiles(ap):
            return ap.rearrange("p (t d) -> p t d", d=D)

        def spread(ap, n):
            return ap.unsqueeze(2).to_broadcast([P, n, D])

        def next_of(b):
            return b[0] + 1, 1 - b[1]

        @block.sync
        def _(sp):
            def load_x(n, t0, t1, s):
                sp.dma_start(tiles(x_of(n, t0, t1)), x_t[bass.ds(n, 1), :, t0:t1].rearrange("o p t d -> p (o t) d")
                             ).then_inc(x_loaded[s], 16)

            def load_adj(n, par, half):
                src = adj_t[bass.ds(n, 1), :, half * HT:(half + 1) * HT, :].rearrange("o p t j -> p (o t) j")
                sp.dma_start(adj_rows[:, 2 * par + half], src).then_inc(adj_loaded[2 * par + half], 16)

            def store(n, half):
                sp.wait_ge(res_ready, 2 * n + half + 1)
                dst = out_t[bass.ds(n, 1), :, half * HT:(half + 1) * HT, :].rearrange("o p t d -> p (o t) d")
                sp.dma_start(dst, tiles(res[:, half])).then_inc(small_moves[half], 16)

            def prologue():
                load_x(0, 0, HT, 0)
                load_x(0, HT, TILES, 1)
                sp.dma_start(w_rows[:, :], w).then_inc(small_moves[0], 16)
                with nc.allow_non_contiguous_dma(reason="a is 256 numbers, turned into two columns"):
                    sp.dma_start(a_cols[:, :], a.rearrange("o (c p) -> p (o c)", p=P)).then_inc(small_moves[1], 16)
                load_x(1, 0, TILES, 3)
                for cols, semaphore in ((slice(0, HN), adj_head_loaded), (slice(HN, N), adj_loaded[0])):
                    sp.dma_start(adj_rows[:, 0, :, cols], adj_t[0, :, 0:HT, cols]).then_inc(semaphore, 16)
                load_adj(0, 0, 1)
                load_adj(1, 1, 0)
                load_adj(1, 1, 1)

            def first(b, after, prep, prev):
                if prev:
                    store(b[0] - 1, 1)

            def second(b, after, ahead):
                if ahead:
                    load_x(ahead[0], 0, TILES, 2 + ahead[1])
                    for half in range(2):
                        sp.wait_ge(edges_ready, 8 * b[0] + 4 * half + 4)
                        load_adj(ahead[0], ahead[1], half)
                store(b[0], 0)

            def epilogue():
                for i in range(HT):
                    sp.wait_ge(last_res, i + 1)
                    sp.dma_start(out_t[BATCHES - 1, :, HT + i], res[:, 1, i * D:(i + 1) * D]).then_inc(last_stored[i], 16)
                sp.wait_ge(small_moves[0], 16 * (BATCHES + 1))
                sp.wait_ge(small_moves[1], 16 * BATCHES)
                for i in range(HT):
                    sp.wait_ge(last_stored[i], 16)

            schedule(sp, first, second, prologue, epilogue)

            def general_tile(n, r, t):
                sp.dma_start(gen_adj, adj_t[bass.ds(n, 1), :, t:t + 1, :].rearrange("o p t j -> p (o t j)")
                             ).then_inc(gen_adj_loaded, 16)
                sp.wait_ge(gen_res_ready, r + 1)
                sp.dma_start(out_t[bass.ds(n, 1), :, t:t + 1, :].rearrange("o p t d -> p (o t d)"), gen_res
                             ).then_inc(small_moves[0], 16)

            def general_end():
                sp.wait_ge(small_moves[0], 16 * (BATCHES + 1 + BATCHES * TILES))

            general_path(sp, None, general_tile, general_end)

        @block.gpsimd
        def _(pool):
            def reciprocal_deviation(count, t0=0, t1=TILES):
                pool.wait_ge(mean_var_ready, count)
                nc.gpsimd.tensor_tensor(var[:, t0:t1], mean_var[:, t0:t1, 1], eps[:, t0:t1], ALU.add
                                        ).then_inc(var_ready, 1)
                pool.wait_ge(var_ready, count)
                nc.gpsimd.tensor_tensor(rstd[:, t0:t1], var[:, t0:t1], neg_half[:, t0:t1], ALU.pow
                                        ).then_inc(rstd_ready, 1)

            def scale_rows(n, par, t0=0, t1=TILES):
                pool.wait_ge(cols_ready, n + 1)
                nc.gpsimd.tensor_tensor(v[:, par, t0:t1], wh[:, t0:t1, 2:2 + NW],
                                        b_col[:, t0:t1].unsqueeze(2).to_broadcast([P, t1 - t0, NW]),
                                        ALU.mult).then_inc(v_ready, 1)

            def divide(n, half):
                pool.wait_ge(rden_ready, 2 * n + half + 1)
                nc.gpsimd.tensor_tensor(tiles(y[:, half]), num[:, half, :, 0:D], spread(rden[:, half], HT),
                                        ALU.mult).then_inc(y_ready, 1)

            def residual(n, half):
                pool.wait_ge(elu_ready, 2 * n + half + 1)
                pool.wait_ge(small_moves[half], 16 * (n + 1))
                nc.gpsimd.tensor_tensor(res[:, half], ey[:, half], x_of(n, half * HT, (half + 1) * HT),
                                        ALU.add).then_inc(res_ready, 1)

            def prologue():
                nc.gpsimd.memset(ident[:, :], 0.0).then_inc(zeroed, 1)
                nc.gpsimd.memset(ones[:, :], 1.0).then_inc(consts_ready, 1)
                nc.gpsimd.memset(neg_half[:, :], -0.5).then_inc(consts_ready, 1)
                nc.gpsimd.memset(eps[:, :], EPS).then_inc(consts_ready, 1)
                nc.gpsimd.memset(shift_f[:, 0:1], -1.0).then_inc(consts_ready, 1)
                nc.gpsimd.memset(shift_f[:, 1:2], FACTOR).then_inc(consts_ready, 1)
                nc.gpsimd.memset(wh[:, :, UW:UW + 1], 1.0).then_inc(consts_ready, 1)
                nc.gpsimd.memset(tiny_row[:, :, D:D + 1], TINY * N).then_inc(consts_ready, 1)
                pool.wait_ge(zeroed, 1)
                nc.gpsimd.affine_select(out=ident[:, :], in_=ident[:, :], compare_op=ALU.not_equal, fill=1.0,
                                        base=0, pattern=[[-1, P]], channel_multiplier=1).then_inc(ident_ready, 1)
                pool.wait_ge(ident_ready, 1)
                nc.gpsimd.tensor_copy(ident_bf[:, :], ident[:, :]).then_inc(ident_ready, 1)
                pool.wait_ge(consts_ready, CONSTANTS)
                for batch in range(2):
                    for half in range(2):
                        reciprocal_deviation(2 * batch + half + 1, half * HT, (half + 1) * HT)
                scale_rows(0, 0, 0, HT)
                scale_rows(0, 0, HT, TILES)

            def first(b, after, prep, prev):
                if prev:
                    divide(b[0] - 1, 1)
                    residual(b[0] - 1, 1)
                if prep:
                    scale_rows(*next_of(b))

            def second(b, after, ahead):
                divide(b[0], 0)
                if ahead:
                    reciprocal_deviation(ahead[0] + 3)
                residual(b[0], 0)

            schedule(pool, first, second, prologue)

            def general_batch(n):
                pool.wait_ge(gen_mean_var, n + 1)
                nc.gpsimd.tensor_tensor(var[:, :], mean_var[:, :, 1], eps[:, :], ALU.add).then_inc(gen_var, 1)
                pool.wait_ge(gen_var, n + 1)
                nc.gpsimd.tensor_tensor(rstd[:, :], var[:, :], neg_half[:, :], ALU.pow).then_inc(gen_rstd, 1)

            general_path(pool, general_batch, None)

        @block.scalar
        def _(act):
            def drain_hT(n, par, half):
                    act.wait_ge(prep_filled, FILLS * n + half + 1)
                    nc.scalar.activation(hT[:, half * HN:(half + 1) * HN], prep[(par + half) % 2][:, :], ACT.Relu,
                                         accum_out=hsum[:, half:half + 1]).then_inc(prep_drained, 1)

            def widen_hsum(n):
                act.wait_ge(prep_drained, FILLS * n + 2)
                nc.scalar.activation(hsum_wide[:, :], ones[:, :], ACT.Identity, scale=hsum[:, 0:1],
                                     bias=hsum[:, 1:2]).then_inc(hsum_ready, 1)

            def drain_wh(n, par):
                for i, (t0, t1) in enumerate(WH_FILLS):
                    f = 2 + i
                    act.wait_ge(prep_filled, FILLS * n + f + 1)
                    src = prep[(par + f) % 2][:, 0:(t1 - t0) * UW].rearrange("p (t c) -> p t c", c=UW)
                    done = nc.scalar.activation(wh[:, t0:t1, 0:UW], src, ACT.Copy)
                    if t1 == TILES:
                        wait(act, num_copied, 4 * (n - 1))
                        o = (t1 - t0) * UW + 2
                        done = nc.scalar.activation(tiny_row[:, par, 0:D], prep[(par + f) % 2][:, o:o + D], ACT.Copy,
                                                    scale=TINY)
                    done.then_inc(prep_drained, 1)

            def exp_columns(n, par):
                act.wait_ge(prep_drained, FILLS * n + FILLS - 2)
                act.wait_ge(shift_ready, n + 1)
                nc.scalar.activation(b_col[:, :], wh[:, :, 1], ACT.Exp, bias=shift[:, 0:1]).then_inc(cols_ready, 1)
                nc.scalar.activation(q_col[:, par], wh[:, :, 1], ACT.Exp, bias=shift[:, 1:2], scale=-FACTOR)

            def exp_rows(n, par, half):
                f = FILLS - 2 + half
                act.wait_ge(prep_filled, FILLS * n + f + 1)
                nc.scalar.activation(g_row[:, par, half * HN:(half + 1) * HN], prep[(par + f) % 2][:, :],
                                     ACT.Exp, bias=shift[:, 1:2], scale=FACTOR).then_inc(prep_drained, 1)

            def mark_edges(b, half, g):
                n, par, rnd = b
                slot = 2 * par + half
                first_load = isinstance(n, int) and n == 0 and half == 0
                if first_load and g < 2:
                    act.wait_ge(adj_head_loaded, 16)
                elif g == 0 or (first_load and g == 2):
                    act.wait_ge(adj_loaded[slot], 16 * (rnd + 1))
                if g == 0:
                    wait(act, adjT_ready, 8 * n + 4 * half - 4)
                cols = slice(2 * g * P, 2 * (g + 1) * P)
                nc.scalar.activation(edges[:, half, :, cols], adj_rows[:, slot, :, cols], ACT.Relu,
                                     scale=LARGE).then_inc(edges_ready, 1)

            def exp_of_negative_part(n, half):
                act.wait_ge(y_ready, 2 * n + half + 1)
                nc.scalar.activation(ey[:, half], y[:, half], ACT.Relu, scale=-1.0).then_inc(neg_ready, 1)
                act.wait_ge(neg_ready, 2 * n + half + 1)
                nc.scalar.activation(ey[:, half], ey[:, half], ACT.Exp, scale=-1.0).then_inc(ey_ready, 1)

            def prologue():
                act.wait_ge(consts_ready, CONSTANTS)
                nc.scalar.activation(rden[:, 0, :], neg_half[:, 0:HT], ACT.Exp).then_inc(warmed, 1)
                drain_hT(0, 0, 0)
                drain_hT(0, 0, 1)
                widen_hsum(0)
                drain_wh(0, 0)
                mark_edges(fixed(0), 0, 0)
                exp_columns(0, 0)
                exp_rows(0, 0, 0)
                for g in range(1, 4):
                    mark_edges(fixed(0), 0, g)
                exp_rows(0, 0, 1)
                for g in range(4):
                    mark_edges(fixed(0), 1, g)

            def first(b, after, prep, prev):
                if prev and after:
                    mark_edges(after, 0, 0)
                if prev:
                    exp_of_negative_part(b[0] - 1, 1)
                if prep:
                    drain_hT(*next_of(b), 0)
                    drain_hT(*next_of(b), 1)
                    widen_hsum(next_of(b)[0])
                if not prev:
                    mark_edges(after, 0, 0)
                if after:
                    mark_edges(after, 0, 1)
                if prep:
                    drain_wh(*next_of(b))
                if after:
                    mark_edges(after, 0, 2)
                    mark_edges(after, 0, 3)

            def second(b, after, ahead):
                if after:
                    exp_columns(after[0], after[1])
                    exp_rows(after[0], after[1], 0)
                    exp_rows(after[0], after[1], 1)
                    mark_edges(after, 1, 0)
                exp_of_negative_part(b[0], 0)
                if after:
                    mark_edges(after, 1, 1)
                    mark_edges(after, 1, 2)
                if after:
                    mark_edges(after, 1, 3)

            def epilogue():
                for i in range(HT):
                    cols = slice(i * D, (i + 1) * D)
                    act.wait_ge(last_y, i + 1)
                    nc.scalar.activation(ey[:, 1, cols], y[:, 1, cols], ACT.Relu, scale=-1.0).then_inc(last_neg, 1)
                    act.wait_ge(last_neg, i + 1)
                    nc.scalar.activation(ey[:, 1, cols], ey[:, 1, cols], ACT.Exp, scale=-1.0).then_inc(last_ey, 1)

            schedule(act, first, second, prologue, epilogue)

            def general_batch(n):
                for half in range(2):
                    act.wait_ge(gen_hT_filled, 2 * n + half + 1)
                    nc.scalar.activation(hT[:, half * HN:(half + 1) * HN], prep[half][:, :], ACT.Relu).then_inc(gen_hT, 1)
                for i, (t0, t1) in enumerate(WH_FILLS):
                    act.wait_ge(gen_wh_filled, len(WH_FILLS) * n + i + 1)
                    src = adjT[i].bitcast(FP32).rearrange("p a i -> p (a i)")[:, 0:(t1 - t0) * UW]
                    nc.scalar.activation(wh[:, t0:t1, 0:UW], src.rearrange("p (t c) -> p t c", c=UW), ACT.Copy
                                         ).then_inc(gen_wh, 1)
                for half in range(2):
                    act.wait_ge(gen_sj_filled, 2 * n + half + 1)
                    nc.scalar.activation(sj_row[:, half * HN:(half + 1) * HN], prep[half][:, :], ACT.Copy
                                         ).then_inc(gen_sj, 1)

            def general_tile(n, r, t):
                act.wait_ge(gen_max_ready, r + 1)
                nc.scalar.activation(gen_p, gen_e, ACT.Exp, bias=gen_max[:, :], accum_out=gen_sum[:, :]
                                     ).then_inc(gen_p_ready, 1)
                for half in range(2):
                    act.wait_ge(gen_pT_filled, 2 * r + half + 1)
                    nc.scalar.activation(gen_pT[:, half * HN:(half + 1) * HN], prep[half][:, :], ACT.Copy
                                         ).then_inc(gen_pT_ready, 1)
                act.wait_ge(gen_y_ready, r + 1)
                nc.scalar.activation(gen_ey, gen_y, ACT.Relu, scale=-1.0).then_inc(gen_neg, 1)
                act.wait_ge(gen_neg, r + 1)
                nc.scalar.activation(gen_ey, gen_ey, ACT.Exp, scale=-1.0).then_inc(gen_ey_ready, 1)

            general_path(act, general_batch, general_tile)

        @block.vector
        def _(dve):
            def row_statistics(n, x_sem, loads, t0=0, t1=TILES):
                dve.wait_ge(x_loaded[x_sem], 16 * loads)
                for t in range(t0, t1):
                    last = nc.vector.bn_stats(stats[:, t], x_of(n, t, t + 1))
                last.then_inc(stats_ready, 1)

            def stats_landed(n):
                dve.wait_ge(stats_ready, n + 3)
                dve.wait_ge(rstd_ready, n + 2)

            def aggregate(t0=0, t1=TILES):
                for t in range(t0, t1):
                    last = nc.vector.bn_aggr(mean_var[:, t], stats[:, t])
                last.then_inc(mean_var_ready, 1)

            def row_moments(batch, half):
                t0, t1, count = half * HT, (half + 1) * HT, 2 * batch + half + 1
                row_statistics(batch, 3 if batch else half, 1, t0, t1)
                dve.wait_ge(stats_ready, count)
                if batch:
                    dve.wait_ge(rstd_ready, count - 2)
                aggregate(t0, t1)

            def normalise(n, half, rstd_count):
                dve.wait_ge(rstd_ready, rstd_count)
                for t in range(half * HT, (half + 1) * HT):
                    done = nc.vector.tensor_scalar(xn[:, t * D:(t + 1) * D], x_of(n, t, t + 1), mean_var[:, t, 0:1],
                                                   rstd[:, t:t + 1], ALU.subtract, ALU.mult)
                done.then_inc(xn_ready, 1)

            def xn_free(n):
                dve.wait_ge(prep_filled, FILLS * (n - 1) + 2)

            def score_maxima(n, par):
                dve.wait_ge(prep_drained, FILLS * n + FILLS - 2)
                nc.vector.tensor_reduce(smax[:, bass.ds(n, 1)], wh[:, :, 0:2], AX.XY, ALU.max,
                                        apply_absolute_value=True)
                nc.vector.tensor_reduce(sjmax[:, :], wh[:, :, 1], AX.X, ALU.max).then_inc(sjmax_ready, 1)

            def score_shift(n, par):
                dve.wait_ge(m_filled, n + 1)
                nc.vector.tensor_reduce(m_all[:, :], prep[(par + FILLS - 1) % 2][:, 0:P], AX.X, ALU.max
                                        ).then_inc(m_ready, 1)
                dve.wait_ge(m_ready, n + 1)
                wait(dve, prep_drained, FILLS * n)
                nc.vector.tensor_scalar(shift[:, :], shift_f[:, :], m_all[:, 0:1], None, ALU.mult).then_inc(shift_ready, 1)

            def edge_weights(b, half, g):
                n, par, _ = b
                q = 8 * n + 4 * half + g
                if g == 0:
                    dve.wait_ge(prep_drained, FILLS * n + FILLS - 1 + half)
                dve.wait_ge(adjT_ready, q + 1)
                for jj in range(2):
                    jt = 2 * g + jj
                    done = nc.vector.scalar_tensor_tensor(
                        weights[:, half, jt], g_row[:, par, half * HN:(half + 1) * HN], q_col[:, par, jt:jt + 1],
                        adjT[g][:, jj], ALU.max, ALU.min)
                done.then_inc(weighted, 1)

            def copy_pair(b, half, pair):
                n, par, _ = b
                dve.wait_ge(num_summed, 4 * n + 2 * half + pair + 1)
                if pair == 0:
                    wait(dve, y_ready, 2 * n + half)
                src = nump[pair][:, 0:2 * NW].rearrange("p (t c) -> p t c", c=NW)
                nc.vector.tensor_tensor(num[:, half, 2 * pair:2 * pair + 2], src,
                                        tiny_row[:, par:par + 1, :].to_broadcast([P, 2, NW]),
                                        ALU.add).then_inc(num_copied, 1)
                if pair == 1:
                    dve.wait_ge(num_copied, 4 * n + 2 * half + 2)
                    nc.vector.reciprocal(rden[:, half], num[:, half, :, D]).then_inc(rden_ready, 1)

            def elu(n, half):
                dve.wait_ge(ey_ready, 2 * n + half + 1)
                nc.vector.scalar_tensor_tensor(ey[:, half], ey[:, half], -1.0, y[:, half],
                                               ALU.add, ALU.max).then_inc(elu_ready, 1)

            def prologue():
                for half in range(2):
                    row_moments(0, half)
                dve.wait_ge(setup_products, 1)
                nc.vector.tensor_copy(u[:, 2:UW], nump[0][:, 0:D]).then_inc(u_ready, 1)
                nc.vector.tensor_copy(u[:, 0:2], nump[1][:, 0:2]).then_inc(u_ready, 1)
                for half in range(2):
                    normalise(0, half, half + 1)
                for half in range(2):
                    row_moments(1, half)
                xn_free(1)
                normalise(1, 0, 3)
                score_maxima(0, 0)
                score_shift(0, 0)
                normalise(1, 1, 4)
                for g in range(4):
                    edge_weights(fixed(0), 0, g)

            def first(b, after, prep, prev):
                edge_weights(b, 1, 0)
                edge_weights(b, 1, 1)
                if prev:
                    elu(b[0] - 1, 1)
                edge_weights(b, 1, 2)
                if prep:
                    score_maxima(*next_of(b))
                if not prep:
                    edge_weights(b, 1, 3)
                copy_pair(b, 0, 0)
                if prep:
                    score_shift(*next_of(b))
                copy_pair(b, 0, 1)
                if prep:
                    edge_weights(b, 1, 3)

            def second(b, after, ahead):
                if ahead:
                    row_statistics(ahead[0], 2 + ahead[1], ahead[1] + ahead[2])
                    stats_landed(ahead[0])
                if after:
                    edge_weights(after, 0, 0)
                if ahead:
                    aggregate()
                if after:
                    edge_weights(after, 0, 1)
                elu(b[0], 0)
                if after:
                    edge_weights(after, 0, 2)
                    copy_pair(b, 1, 0)
                    copy_pair(b, 1, 1)
                if ahead:
                    xn_free(ahead[0])
                    for half in range(2):
                        normalise(ahead[0], half, ahead[0] + 3)
                if after:
                    edge_weights(after, 0, 3)

            def epilogue():
                dve.wait_ge(y_ready, 2 * BATCHES - 1)
                dve.wait_ge(small_moves[1], 16 * BATCHES)

                def average(i):
                    dve.wait_ge(last_summed, i + 1)
                    nc.vector.tensor_tensor(num[:, 1, i], nump[i % 2][:, 0:NW], tiny_row[:, (BATCHES - 1) % 2], ALU.add
                                            ).then_inc(last_copied, 1)
                    dve.wait_ge(last_copied, i + 1)
                    nc.vector.reciprocal(rden[:, 1, i:i + 1], num[:, 1, i, D:NW]).then_inc(last_rden, 1)
                    dve.wait_ge(last_rden, i + 1)
                    nc.vector.tensor_scalar(y[:, 1, i * D:(i + 1) * D], num[:, 1, i, 0:D], rden[:, 1, i:i + 1], None,
                                            ALU.mult).then_inc(last_y, 1)

                def finish(i):
                    cols = slice(i * D, (i + 1) * D)
                    dve.wait_ge(last_ey, i + 1)
                    nc.vector.scalar_tensor_tensor(ey[:, 1, cols], ey[:, 1, cols], -1.0, y[:, 1, cols],
                                                   ALU.add, ALU.max).then_inc(last_elu, 1)
                    dve.wait_ge(last_elu, i + 1)
                    nc.vector.tensor_tensor(res[:, 1, cols], ey[:, 1, cols], x_of(BATCHES - 1, HT + i, HT + i + 1),
                                            ALU.add).then_inc(last_res, 1)

                average(0)
                for i in range(1, HT):
                    average(i)
                    finish(i - 1)
                finish(HT - 1)

            def largest_score():
                dve.wait_ge(sjmax_ready, BATCHES)
                nc.vector.tensor_reduce(smax_all[:, :], smax[:, :], AX.X, ALU.max).then_inc(smax_ready, 1)

            def choose_path():
                dve.wait_ge(smax_filled, 1)
                nc.vector.tensor_reduce(smax_all[:, :], prep[0][:, 0:P], AX.X, ALU.max).then_inc(smax_known, 1)
                dve.wait_ge(smax_known, 1)
                nc.vector.tensor_scalar(unsafe[:, :], smax_all[:, :], SAFE_SCORE, None, ALU.is_gt).then_inc(unsafe_ready, 1)

            schedule(dve, first, second, prologue, epilogue, largest_score, choose_path)

            def general_batch(n):
                dve.wait_ge(small_moves[0], 16 * (BATCHES + 1))
                dve.wait_ge(small_moves[1], 16 * BATCHES)
                for i in range(HT):
                    dve.wait_ge(last_stored[i], 16)
                for t in range(TILES):
                    last = nc.vector.bn_stats(stats[:, t], x_of(n, t, t + 1))
                last.then_inc(gen_stats, 1)
                dve.wait_ge(gen_stats, n + 1)
                nc.vector.memset(gen_scratch[:, :], 0.0)
                for t in range(TILES):
                    last = nc.vector.bn_aggr(mean_var[:, t], stats[:, t])
                last.then_inc(gen_mean_var, 1)
                dve.wait_ge(gen_rstd, n + 1)
                for t in range(TILES):
                    last = nc.vector.tensor_scalar(xn[:, t * D:(t + 1) * D], x_of(n, t, t + 1), mean_var[:, t, 0:1],
                                                   rstd[:, t:t + 1], ALU.subtract, ALU.mult)
                last.then_inc(gen_xn, 1)

            def general_tile(n, r, t):
                def chained(step):
                    dve.wait_ge(gen_chain, CHAIN * r + step)

                dve.wait_ge(gen_sj, 2 * n + 2)
                nc.vector.tensor_scalar(gen_e, sj_row, wh[:, t, 0:1], None, ALU.add).then_inc(gen_chain, 1)
                chained(1)
                nc.vector.scalar_tensor_tensor(gen_e, gen_e, ALPHA, gen_e, ALU.mult, ALU.max).then_inc(gen_chain, 1)
                dve.wait_ge(gen_adj_loaded, 16 * (r + 1))
                nc.vector.tensor_scalar(gen_mask, gen_adj, 0.0, None, ALU.is_gt).then_inc(gen_chain, 1)
                chained(3)
                nc.vector.tensor_scalar(gen_off, gen_mask, 1.0, -NO_EDGE, ALU.subtract, ALU.mult).then_inc(gen_chain, 1)
                nc.vector.tensor_tensor(gen_e, gen_e, gen_mask, ALU.mult).then_inc(gen_chain, 1)
                chained(5)
                nc.vector.tensor_tensor(gen_e, gen_e, gen_off, ALU.add).then_inc(gen_off_added, 1)
                dve.wait_ge(gen_off_added, r + 1)
                nc.vector.tensor_reduce(gen_max[:, :], gen_e, AX.X, ALU.max, negate=True).then_inc(gen_max_ready, 1)
                dve.wait_ge(gen_p_ready, r + 1)
                nc.vector.reciprocal(gen_inv[:, :], gen_sum[:, :]).then_inc(gen_inv_ready, 1)
                dve.wait_ge(gen_inv_ready, r + 1)
                dve.wait_ge(gen_summed, r + 1)
                nc.vector.tensor_scalar(gen_y, nump[0][:, 0:D], gen_inv[:, 0:1], None, ALU.mult).then_inc(gen_y_ready, 1)
                dve.wait_ge(gen_ey_ready, r + 1)
                nc.vector.scalar_tensor_tensor(gen_ey, gen_ey, -1.0, gen_y, ALU.add, ALU.max).then_inc(gen_elu, 1)
                dve.wait_ge(gen_elu, r + 1)
                dve.wait_ge(small_moves[0], 16 * (BATCHES + 1 + r))
                nc.vector.tensor_tensor(gen_res, gen_ey, x_of(n, t, t + 1), ALU.add).then_inc(gen_res_ready, 1)

            general_path(dve, general_batch, general_tile)

        @block.tensor
        def _(pe):
            def open_fill(n, f):
                wait(pe, prep_drained, FILLS * n + f - 1)

            def fill_hT(n, par, half):
                pe.wait_ge(xn_ready, 2 * n + half + 1)
                open_fill(n, half)
                for t in range(HT):
                    last = nc.tensor.transpose(prep[(par + half) % 2][:, t * P:(t + 1) * P],
                                               xn[:, (half * HT + t) * D:(half * HT + t + 1) * D], ident[:, :])
                last.then_inc(prep_filled, 1)

            def fill_wh(n, par, i):
                f = 2 + i
                t0, t1 = WH_FILLS[i]
                open_fill(n, f)
                pe.wait_ge(prep_drained, FILLS * n + (1 if t1 <= HT else 2))
                bank = prep[(par + f) % 2]
                for t in range(t0, t1):
                    last = nc.tensor.matmul(bank[:, (t - t0) * UW:(t - t0 + 1) * UW], hT[:, t * P:(t + 1) * P], u[:, :],
                                            start=True, stop=True)
                if t1 == TILES:
                    pe.wait_ge(hsum_ready, n + 1)
                    last = nc.tensor.matmul(bank[:, (t1 - t0) * UW:(t1 - t0 + 1) * UW], hsum_wide[:, :], u[:, :],
                                            start=True, stop=True)
                last.then_inc(prep_filled, 1)

            def fill_m(n, par):
                pe.wait_ge(sjmax_ready, n + 1)
                nc.tensor.transpose(prep[(par + FILLS - 1) % 2][:, 0:P], sjmax[:, 0:1].to_broadcast([P, P]),
                                    ident[:, :]).then_inc(m_filled, 1)

            def fill_si(n, par, half):
                f = FILLS - 2 + half
                open_fill(n, f)
                if half:
                    pe.wait_ge(m_ready, n + 1)
                for t in range(HT):
                    last = nc.tensor.transpose(prep[(par + f) % 2][:, t * P:(t + 1) * P],
                                               wh[:, half * HT + t, 0:1].to_broadcast([P, P]), ident[:, :])
                last.then_inc(prep_filled, 1)

            def transpose_group(b, half, g):
                q = 8 * b[0] + 4 * half + g
                pe.wait_ge(edges_ready, q + 1)
                wait(pe, weighted, q - 3)
                for jj in range(2):
                    jt = 2 * g + jj
                    for t in range(HT):
                        last = nc.tensor.transpose(adjT[g][:, jj, t * P:(t + 1) * P],
                                                   edges[:, half, t, jt * P:(jt + 1) * P], ident_bf[:, :])
                last.then_inc(adjT_ready, 1)

            def sum_quarter(b, half, quarter):
                n, par, _ = b
                odd = quarter // 2

                def add(i, jts):
                    for jt in jts:
                        last = nc.tensor.matmul(nump[i // 2][:, (i % 2) * NW:(i % 2 + 1) * NW],
                                                weights[:, half, jt, i * P:(i + 1) * P], v[:, par, jt],
                                                start=jt == 0, stop=jt == TILES - 1)
                    return last

                j0 = HT * (quarter % 2)
                if odd:
                    for i in (1, 3):
                        last = add(i, range(j0, j0 + HT))
                        if quarter == 3:
                            last.then_inc(num_summed, 1)
                    return
                for g in (j0 // 2, j0 // 2 + 1):
                    pe.wait_ge(weighted, 8 * n + 4 * half + g + 1)
                    if isinstance(n, int) and n == 0:
                        pe.wait_ge(v_ready, 1 + g // 2)
                    elif g == 0:
                        pe.wait_ge(v_ready, n + 2)
                    for i in (0, 2):
                        if g == 0:
                            wait(pe, num_copied, 4 * n + 2 * half + i // 2 - 1)
                        add(i, (2 * g, 2 * g + 1))

            def sum_last_tile(i):
                if i == 0:
                    pe.wait_ge(weighted, 8 * BATCHES)
                if i < 2:
                    pe.wait_ge(num_copied, 4 * BATCHES - 3 + i)
                else:
                    pe.wait_ge(last_copied, i - 1)
                for jt in range(TILES):
                    last = nc.tensor.matmul(nump[i % 2][:, 0:NW], weights[:, 1, jt, i * P:(i + 1) * P],
                                            v[:, (BATCHES - 1) % 2, jt], start=jt == 0, stop=jt == TILES - 1)
                last.then_inc(last_summed, 1)

            def warm(count):
                for _ in range(count):
                    last = nc.tensor.matmul(adjT[0].bitcast(FP32).rearrange("p a i -> p (a i)")[:, 0:P], ident[:, :],
                                            ident[:, :], start=True, stop=True)
                last.then_inc(warmed, 1)

            def prologue():
                pe.wait_ge(ident_ready, 2)
                warm(5)
                pe.wait_ge(small_moves[0], 16)
                pe.wait_ge(small_moves[1], 16)
                nc.tensor.transpose(nump[0][:, 0:D], w_rows[:, :], ident[:, :])
                nc.tensor.matmul(nump[1][:, 0:2], w_rows[:, :], a_cols[:, :], start=True, stop=True
                                 ).then_inc(setup_products, 1)
                warm(6)
                fill_hT(0, 0, 0)
                fill_hT(0, 0, 1)
                pe.wait_ge(u_ready, 2)
                fill_wh(0, 0, 0)
                fill_wh(0, 0, 1)
                fill_wh(0, 0, 2)
                fill_m(0, 0)
                fill_si(0, 0, 0)
                fill_si(0, 0, 1)
                transpose_group(fixed(0), 0, 0)
                transpose_group(fixed(0), 0, 1)
                transpose_group(fixed(0), 0, 2)

            def first(b, after, prep, prev):
                m = next_of(b)
                if prev:
                    transpose_group(b, 1, 0)
                sum_quarter(b, 0, 0)
                if not prev:
                    transpose_group(b, 0, 3)
                else:
                    transpose_group(b, 1, 1)
                if prep:
                    fill_hT(*m, 0)
                    fill_hT(*m, 1)
                if not prev:
                    transpose_group(b, 1, 0)
                    transpose_group(b, 1, 1)
                sum_quarter(b, 0, 1)
                transpose_group(b, 1, 2)
                if prep:
                    fill_wh(*m, 0)
                    fill_wh(*m, 1)
                sum_quarter(b, 0, 2)
                transpose_group(b, 1, 3)
                if prep:
                    fill_wh(*m, 2)
                sum_quarter(b, 0, 3)
                if prep:
                    fill_m(*m)
                    fill_si(*m, 0)
                    fill_si(*m, 1)

            def second(b, after, ahead):
                if after:
                    for g in range(4):
                        transpose_group(after, 0, g)
                        sum_quarter(b, 1, g)
                else:
                    for i in range(HT):
                        sum_last_tile(i)

            def spread_smax():
                pe.wait_ge(smax_ready, 1)
                pe.wait_ge(prep_drained, FILLS * BATCHES)
                nc.tensor.transpose(prep[0][:, 0:P], smax_all[:, 0:1].to_broadcast([P, P]), ident[:, :]
                                    ).then_inc(smax_filled, 1)

            schedule(pe, first, second, prologue, after_preparation=spread_smax)

            def general_batch(n):
                pe.wait_ge(gen_xn, n + 1)
                for half in range(2):
                    for t in range(HT):
                        last = nc.tensor.transpose(prep[half][:, t * P:(t + 1) * P],
                                                   xn[:, (half * HT + t) * D:(half * HT + t + 1) * D], ident[:, :])
                    last.then_inc(gen_hT_filled, 1)
                pe.wait_ge(gen_hT, 2 * n + 2)
                for i, (t0, t1) in enumerate(WH_FILLS):
                    bank = adjT[i].bitcast(FP32).rearrange("p a i -> p (a i)")
                    for t in range(t0, t1):
                        last = nc.tensor.matmul(bank[:, (t - t0) * UW:(t - t0 + 1) * UW], hT[:, t * P:(t + 1) * P],
                                                u[:, :], start=True, stop=True)
                    last.then_inc(gen_wh_filled, 1)
                pe.wait_ge(gen_wh, len(WH_FILLS) * (n + 1))
                for half in range(2):
                    for t in range(HT):
                        last = nc.tensor.transpose(prep[half][:, t * P:(t + 1) * P],
                                                   wh[:, half * HT + t, 1:2].to_broadcast([P, P]), ident[:, :])
                    last.then_inc(gen_sj_filled, 1)

            def general_tile(n, r, t):
                pe.wait_ge(gen_sj, 2 * n + 2)
                pe.wait_ge(gen_p_ready, r + 1)
                for half in range(2):
                    for jj in range(HT):
                        jt = half * HT + jj
                        last = nc.tensor.transpose(prep[half][:, jj * P:(jj + 1) * P], gen_p[:, jt * P:(jt + 1) * P],
                                                   ident[:, :])
                    last.then_inc(gen_pT_filled, 1)
                pe.wait_ge(gen_pT_ready, 2 * r + 2)
                for jt in range(TILES):
                    last = nc.tensor.matmul(nump[0][:, 0:D], gen_pT[:, jt * P:(jt + 1) * P], wh[:, jt, 2:2 + D],
                                            start=jt == 0, stop=jt == TILES - 1)
                last.then_inc(gen_summed, 1)

            general_path(pe, general_batch, general_tile)


def kernel(x, adj, L0_gnn_W, L0_gnn_a):
    import numpy as np
    import concourse.bacc as bacc
    from concourse.bass_utils import run_bass_kernel_spmd

    nc = bacc.Bacc("TRN2", target_bir_lowering=False, num_devices=1)
    arrays, args = {}, []
    for name, value in (("x", x), ("adj", adj), ("w", L0_gnn_W), ("a", L0_gnn_a)):
        value = np.ascontiguousarray(value)
        arrays[f"in_{name}"] = value
        args.append(nc.dram_tensor(f"in_{name}", value.shape, mybir.dt.from_np(value.dtype), kind="ExternalInput").ap())
    args.append(nc.dram_tensor("out", x.shape, FP32, kind="ExternalOutput").ap())
    graph_attention_kernel(nc, *args)
    r = run_bass_kernel_spmd(nc, [arrays], core_ids=[0])
    return r.results[0]["out"]
```
